# Optimizing a Trainium2 kernel written in Bass

```python
import numpy as np
import jax
import jax.numpy as jnp

def _softmax(x, axis=-1):
    return jax.nn.softmax(x, axis=axis)

def _gelu(x):
    return jax.nn.gelu(x, approximate=True)

def _silu(x):
    return jax.nn.silu(x)

def _sigmoid(x):
    return jax.nn.sigmoid(x)

def _layernorm(x, axis=-1, eps=1e-05):
    m = jnp.mean(x, axis=axis, keepdims=True)
    v = jnp.var(x, axis=axis, keepdims=True)
    return (x - m) / jnp.sqrt(v + eps)

def _scatter_add(tgt, idx, src, axis=0):
    return tgt.at[idx].add(src)

def _segment_sum(src, seg, n):
    return jax.ops.segment_sum(src, seg, n)
kernel_name = 'mk_seq_postln_d1_jaxref_r4_c762b7'

def setup_inputs(seed: int=0):
    np.random.seed(seed)
    _w = jnp.asarray

    def _L0_attn_setup():
        import jax, jax.numpy as jnp
        import numpy as np
        B, T, D = (1, 512, 256)
        H, DH, DV, DF = (16, 64, 64, 1024)
        EPS_LN = 1e-05
        EPS_DEN = 1e-06

        def _layernorm(x, g, b):
            m = jnp.mean(x, axis=-1, keepdims=True)
            v = jnp.mean((x - m) ** 2, axis=-1, keepdims=True)
            return (x - m) / jnp.sqrt(v + EPS_LN) * g + b

        def _phi(x):
            return jax.nn.elu(x) + 1.0

        def _linear_attention(x, Wq, Wk, Wv, Wo):
            b, t, d = x.shape
            Q = _phi((x @ Wq).reshape(b, t, H, DH)).transpose(0, 2, 1, 3)
            K = _phi((x @ Wk).reshape(b, t, H, DH)).transpose(0, 2, 1, 3)
            V = (x @ Wv).reshape(b, t, H, DV).transpose(0, 2, 1, 3)
            KV = jnp.einsum('bhti,bhtj->bhtij', K, V)
            S = jnp.cumsum(KV, axis=2)
            z = jnp.cumsum(K, axis=2)
            num = jnp.einsum('bhti,bhtij->bhtj', Q, S)
            den = jnp.maximum(jnp.einsum('bhti,bhti->bht', Q, z), EPS_DEN)[..., None]
            out = (num / den).transpose(0, 2, 1, 3).reshape(b, t, H * DV)
            return out @ Wo
        key = jax.random.key(seed)
        ks = jax.random.split(key, 8)
        s = 0.02
        return {'x': jax.random.normal(ks[0], (B, T, D), dtype=jnp.float32), 'ln1_g': jnp.ones((D,), jnp.float32), 'ln1_b': jnp.zeros((D,), jnp.float32), 'Wq': jax.random.normal(ks[1], (D, H * DH), jnp.float32) * s, 'Wk': jax.random.normal(ks[2], (D, H * DH), jnp.float32) * s, 'Wv': jax.random.normal(ks[3], (D, H * DV), jnp.float32) * s, 'Wo': jax.random.normal(ks[4], (H * DV, D), jnp.float32) * s, 'ln2_g': jnp.ones((D,), jnp.float32), 'ln2_b': jnp.zeros((D,), jnp.float32), 'Wf1': jax.random.normal(ks[5], (D, DF), jnp.float32) * s, 'Wf2': jax.random.normal(ks[6], (DF, D), jnp.float32) * s}
    _L0_attn_in = _L0_attn_setup()

    def _L0_ffn_setup():
        import jax, jax.numpy as jnp
        import numpy as np
        import math
        D = 256
        H = 16
        E = 8
        TOPK = 2
        LAT = D // 2
        KPH = LAT // H
        HD = D // H

        def _forward(hs, q_w, q_b, k_w, k_b, v_w, v_b, o_w, o_b, router_w, router_b, w1, b1, w2, b2):
            B, S, _ = hs.shape
            Q = (hs @ q_w + q_b).reshape(B, S, H, HD).transpose(0, 2, 1, 3)
            K = (hs @ k_w + k_b).reshape(B, S, H, KPH).transpose(0, 2, 1, 3)
            V = (hs @ v_w + v_b).reshape(B, S, H, KPH).transpose(0, 2, 1, 3)
            scores = jnp.einsum('bhsk,bhtk->bhst', Q[..., :KPH], K) / math.sqrt(KPH)
            attn = jax.nn.softmax(scores, axis=-1)
            ao = jnp.einsum('bhst,bhtv->bhsv', attn, V)
            ao = ao.transpose(0, 2, 1, 3).reshape(B, S, H * KPH)
            ao = jnp.concatenate([ao, jnp.zeros((B, S, D - LAT), ao.dtype)], axis=-1)
            mla_out = ao @ o_w + o_b
            probs = jax.nn.softmax(mla_out @ router_w + router_b, axis=-1)
            topw, topi = jax.lax.top_k(probs, TOPK)
            topw = topw / (topw.sum(-1, keepdims=True) + 1e-08)
            combine = jnp.sum(jax.nn.one_hot(topi, E, dtype=probs.dtype) * topw[..., None], axis=-2)
            h1 = jnp.einsum('bsd,edf->ebsf', mla_out, w1) + b1[:, None, None, :]
            h1 = jax.nn.gelu(h1, approximate=False)
            h2 = jnp.einsum('ebsf,efd->ebsd', h1, w2) + b2[:, None, None, :]
            moe_out = jnp.einsum('bse,ebsd->bsd', combine, h2)
            return hs + 0.3 * moe_out
        key = jax.random.key(seed)
        ks = jax.random.split(key, 16)
        s = 0.02
        inp = {'hidden_states': jax.random.normal(ks[0], (2, 512, D), jnp.float32), 'q_w': jax.random.normal(ks[1], (D, D), jnp.float32) * s, 'q_b': jnp.zeros((D,), jnp.float32), 'k_w': jax.random.normal(ks[2], (D, LAT), jnp.float32) * s, 'k_b': jnp.zeros((LAT,), jnp.float32), 'v_w': jax.random.normal(ks[3], (D, LAT), jnp.float32) * s, 'v_b': jnp.zeros((LAT,), jnp.float32), 'o_w': jax.random.normal(ks[4], (D, D), jnp.float32) * s, 'o_b': jnp.zeros((D,), jnp.float32), 'router_w': jax.random.normal(ks[5], (D, E), jnp.float32) * s, 'router_b': jnp.zeros((E,), jnp.float32), 'w1': jax.random.normal(ks[6], (E, D, 2 * D), jnp.float32) * s, 'b1': jnp.zeros((E, 2 * D), jnp.float32), 'w2': jax.random.normal(ks[7], (E, 2 * D, D), jnp.float32) * s, 'b2': jnp.zeros((E, D), jnp.float32)}
        return inp
    _L0_ffn_in = _L0_ffn_setup()
    _d = {'L0_attn_x': _L0_attn_in['x'], 'L0_attn_ln1_g': _L0_attn_in['ln1_g'], 'L0_attn_ln1_b': _L0_attn_in['ln1_b'], 'L0_attn_Wq': _L0_attn_in['Wq'], 'L0_attn_Wk': _L0_attn_in['Wk'], 'L0_attn_Wv': _L0_attn_in['Wv'], 'L0_attn_Wo': _L0_attn_in['Wo'], 'L0_attn_ln2_g': _L0_attn_in['ln2_g'], 'L0_attn_ln2_b': _L0_attn_in['ln2_b'], 'L0_attn_Wf1': _L0_attn_in['Wf1'], 'L0_attn_Wf2': _L0_attn_in['Wf2'], 'L0_ffn_q_w': _L0_ffn_in['q_w'], 'L0_ffn_q_b': _L0_ffn_in['q_b'], 'L0_ffn_k_w': _L0_ffn_in['k_w'], 'L0_ffn_k_b': _L0_ffn_in['k_b'], 'L0_ffn_v_w': _L0_ffn_in['v_w'], 'L0_ffn_v_b': _L0_ffn_in['v_b'], 'L0_ffn_o_w': _L0_ffn_in['o_w'], 'L0_ffn_o_b': _L0_ffn_in['o_b'], 'L0_ffn_router_w': _L0_ffn_in['router_w'], 'L0_ffn_router_b': _L0_ffn_in['router_b'], 'L0_ffn_w1': _L0_ffn_in['w1'], 'L0_ffn_b1': _L0_ffn_in['b1'], 'L0_ffn_w2': _L0_ffn_in['w2'], 'L0_ffn_b2': _L0_ffn_in['b2']}
    _x0 = _d['L0_attn_x']
    _d['L0_attn_x'] = jax.random.normal(jax.random.fold_in(jax.random.key(seed), 1), (2, 2048, 256), dtype=_x0.dtype)
    del _x0
    return _d

def reference(L0_attn_x, L0_attn_ln1_g, L0_attn_ln1_b, L0_attn_Wq, L0_attn_Wk, L0_attn_Wv, L0_attn_Wo, L0_attn_ln2_g, L0_attn_ln2_b, L0_attn_Wf1, L0_attn_Wf2, L0_ffn_q_w, L0_ffn_q_b, L0_ffn_k_w, L0_ffn_k_b, L0_ffn_v_w, L0_ffn_v_b, L0_ffn_o_w, L0_ffn_o_b, L0_ffn_router_w, L0_ffn_router_b, L0_ffn_w1, L0_ffn_b1, L0_ffn_w2, L0_ffn_b2):

    def _L0_attn_ref(x, ln1_g, ln1_b, Wq, Wk, Wv, Wo, ln2_g, ln2_b, Wf1, Wf2):
        import jax, jax.numpy as jnp
        import numpy as np
        B, T, D = (1, 512, 256)
        H, DH, DV, DF = (16, 64, 64, 1024)
        EPS_LN = 1e-05
        EPS_DEN = 1e-06

        def _layernorm(x, g, b):
            m = jnp.mean(x, axis=-1, keepdims=True)
            v = jnp.mean((x - m) ** 2, axis=-1, keepdims=True)
            return (x - m) / jnp.sqrt(v + EPS_LN) * g + b

        def _phi(x):
            return jax.nn.elu(x) + 1.0

        def _linear_attention(x, Wq, Wk, Wv, Wo):
            b, t, d = x.shape
            Q = _phi((x @ Wq).reshape(b, t, H, DH)).transpose(0, 2, 1, 3)
            K = _phi((x @ Wk).reshape(b, t, H, DH)).transpose(0, 2, 1, 3)
            V = (x @ Wv).reshape(b, t, H, DV).transpose(0, 2, 1, 3)
            KV = jnp.einsum('bhti,bhtj->bhtij', K, V)
            S = jnp.cumsum(KV, axis=2)
            z = jnp.cumsum(K, axis=2)
            num = jnp.einsum('bhti,bhtij->bhtj', Q, S)
            den = jnp.maximum(jnp.einsum('bhti,bhti->bht', Q, z), EPS_DEN)[..., None]
            out = (num / den).transpose(0, 2, 1, 3).reshape(b, t, H * DV)
            return out @ Wo
        x = x + _linear_attention(_layernorm(x, ln1_g, ln1_b), Wq, Wk, Wv, Wo)
        h = _layernorm(x, ln2_g, ln2_b)
        x = x + jax.nn.gelu(h @ Wf1, approximate=False) @ Wf2
        return x

    def _L0_ffn_ref(hidden_states, q_w, q_b, k_w, k_b, v_w, v_b, o_w, o_b, router_w, router_b, w1, b1, w2, b2):
        import jax, jax.numpy as jnp
        import numpy as np
        import math
        D = 256
        H = 16
        E = 8
        TOPK = 2
        LAT = D // 2
        KPH = LAT // H
        HD = D // H

        def _forward(hs, q_w, q_b, k_w, k_b, v_w, v_b, o_w, o_b, router_w, router_b, w1, b1, w2, b2):
            B, S, _ = hs.shape
            Q = (hs @ q_w + q_b).reshape(B, S, H, HD).transpose(0, 2, 1, 3)
            K = (hs @ k_w + k_b).reshape(B, S, H, KPH).transpose(0, 2, 1, 3)
            V = (hs @ v_w + v_b).reshape(B, S, H, KPH).transpose(0, 2, 1, 3)
            scores = jnp.einsum('bhsk,bhtk->bhst', Q[..., :KPH], K) / math.sqrt(KPH)
            attn = jax.nn.softmax(scores, axis=-1)
            ao = jnp.einsum('bhst,bhtv->bhsv', attn, V)
            ao = ao.transpose(0, 2, 1, 3).reshape(B, S, H * KPH)
            ao = jnp.concatenate([ao, jnp.zeros((B, S, D - LAT), ao.dtype)], axis=-1)
            mla_out = ao @ o_w + o_b
            probs = jax.nn.softmax(mla_out @ router_w + router_b, axis=-1)
            topw, topi = jax.lax.top_k(probs, TOPK)
            topw = topw / (topw.sum(-1, keepdims=True) + 1e-08)
            combine = jnp.sum(jax.nn.one_hot(topi, E, dtype=probs.dtype) * topw[..., None], axis=-2)
            h1 = jnp.einsum('bsd,edf->ebsf', mla_out, w1) + b1[:, None, None, :]
            h1 = jax.nn.gelu(h1, approximate=False)
            h2 = jnp.einsum('ebsf,efd->ebsd', h1, w2) + b2[:, None, None, :]
            moe_out = jnp.einsum('bse,ebsd->bsd', combine, h2)
            return hs + 0.3 * moe_out
        return _forward(hidden_states, q_w, q_b, k_w, k_b, v_w, v_b, o_w, o_b, router_w, router_b, w1, b1, w2, b2)
    x = L0_attn_x
    x = _layernorm(x + _L0_attn_ref(x, L0_attn_ln1_g, L0_attn_ln1_b, L0_attn_Wq, L0_attn_Wk, L0_attn_Wv, L0_attn_Wo, L0_attn_ln2_g, L0_attn_ln2_b, L0_attn_Wf1, L0_attn_Wf2), axis=-1)
    x = _layernorm(x + _L0_ffn_ref(x, L0_ffn_q_w, L0_ffn_q_b, L0_ffn_k_w, L0_ffn_k_b, L0_ffn_v_w, L0_ffn_v_b, L0_ffn_o_w, L0_ffn_o_b, L0_ffn_router_w, L0_ffn_router_b, L0_ffn_w1, L0_ffn_b1, L0_ffn_w2, L0_ffn_b2), axis=-1)
    return x

_drawn_inputs = setup_inputs


def setup_inputs(seed=0):
    import zlib

    import numpy as np

    out = dict(_drawn_inputs(seed))
    spreads = {'L0_attn_ln1_g': (1.0, 0.6),
     'L0_attn_ln1_b': (0.0, 0.8),
     'L0_attn_ln2_g': (1.0, 0.6),
     'L0_attn_ln2_b': (0.0, 2.0),
     'L0_ffn_q_b': (0.0, 0.8),
     'L0_ffn_k_b': (0.0, 2.0),
     'L0_ffn_v_b': (0.0, 0.8),
     'L0_ffn_o_b': (0.0, 0.757),
     'L0_ffn_router_b': (0.0, 2.0),
     'L0_ffn_b1': (0.0, 0.8),
     'L0_ffn_b2': (0.0, 2.0)}
    factors = {'L0_attn_Wq': 8.0,
     'L0_attn_Wk': 8.0,
     'L0_attn_Wv': 4.774,
     'L0_attn_Wo': 4.676,
     'L0_ffn_q_w': 8.0,
     'L0_ffn_k_w': 8.0,
     'L0_ffn_v_w': 8.0,
     'L0_ffn_o_w': 8.0,
     'L0_ffn_router_w': 7.428,
     'L0_ffn_w1': 8.0,
     'L0_ffn_w2': 8.0}
    for name, (base, spread) in spreads.items():
        noise = np.random.default_rng([zlib.crc32(name.encode()), seed]).standard_normal(out[name].shape)
        drawn = base * np.exp(spread * noise) if base else spread * noise
        out[name] = jnp.asarray(drawn.astype(out[name].dtype))
    for name, factor in factors.items():
        out[name] = (out[name] * factor).astype(out[name].dtype)
    return out
```

```python
from contextlib import ExitStack

import concourse.bass as bass
from concourse import mybir

F32 = mybir.dt.float32
BF16 = mybir.dt.bfloat16
U32 = mybir.dt.uint32
ACT = mybir.ActivationFunctionType
ALU = mybir.AluOpType
AX = mybir.AxisListType

P = 128
B, T, D = 2, 2048, 256
N = B * T
ST = 512
NT = ST // P
STEPS = N // ST
DC = D // P
H = 16
DH = 64
PAIRS = H // 2
DF = 1024
FC = DF // P
LAT = D // 2
KPH = LAT // H
VW = KPH + 1
PARTS = 3
E = 8
EF = 2 * D
EC = EF // P
EPS_LN = 1e-5
EPS_DEN = 1e-6


def identity_matrix(eng, tile, done):
    eng.memset(tile, 0.0).then_inc(done, 1)
    eng.wait_ge(done, 1)
    eng.affine_select(out=tile, in_=tile, compare_op=ALU.not_equal, fill=1.0, base=0,
                      pattern=[[-1, P]], channel_multiplier=1).then_inc(done, 1)


def from_one(eng, *sems):
    for sem in sems:
        eng.sem_inc(sem, 1)


def wait_apart(eng, sem, value, passed):
    eng.wait_ge(sem, value)
    eng.sem_inc(passed, 1)


class Steps:

    def __init__(self, sem, per):
        self.sem, self.per, self.n = sem, per, 0

    def mark(self, instruction):
        self.n += 1
        instruction.then_inc(self.sem, 1)

    def value(self, g):
        return g * self.per + self.n


def linear_attention_stage(nc, a, scratch):
    ctx = ExitStack()
    with ctx:
        def sb(name, shape, dt=F32):
            return ctx.enter_context(nc.sbuf_tensor(name, shape, dt))

        def bank(name):
            return ctx.enter_context(nc.psum_tensor(name, [P, 512], F32))

        def sem(name):
            return ctx.enter_context(nc.semaphore(name))

        wq, wk, wv = (sb(n, [P, DC, H * DH]) for n in ("wq", "wk", "wv"))
        wo = sb("wo", [P, PAIRS, D])
        wf1 = sb("wf1", [P, DC, DF])
        wf2 = sb("wf2", [P, FC, D])
        qw, kw, vw = (sb(n, [P, DC, LAT]) for n in ("qw", "kw", "vw"))
        ln1g, ln1b, ln2g, ln2b = (sb(n, [P, DC]) for n in ("ln1g", "ln1b", "ln2g", "ln2b"))
        qb, kb = sb("qb", [LAT, 1]), sb("kb", [LAT, 1])
        vb = sb("vb", [P, LAT])
        ident = sb("ident", [P, P])
        causal = sb("causal", [P, 4, P])
        keep = sb("keep", [P, STEPS])
        ones = sb("ones", [P, DH])
        minus_half = sb("minus_half", [P, NT])
        x = sb("x", [P, STEPS * NT, D])
        xn = sb("xn", [P, NT, D])
        feat = sb("feat", [P, DC, ST])
        stats = sb("stats", [P, NT, 6])
        meanvar = sb("meanvar", [P, NT, 2])
        var_eps = sb("var_eps", [P, NT])
        rstd = sb("rstd", [P, NT])
        ex = sb("ex", [P, 2, ST])
        qT = sb("qT", [P, PAIRS, 2, ST])
        kT = sb("kT", [P, PAIRS, ST])
        fT = kT
        kt = sb("kt", [P, H, DH])
        vt = sb("vt", [P, H, 2, DH])
        att = sb("att", [P, H, P])
        den = sb("den", [P, ST])
        oT = sb("oT", [P, PAIRS, P])
        state = sb("state", [P, 2, PAIRS, 2 * DH])
        x1 = sb("x1", [P, NT, D])
        y = x1
        x3 = sb("x3", [P, NT, D])
        qk = sb("qk", [P, 2, ST])
        rest = sb("rest", [P, 2, ST])
        parts = sb("parts", [P, 2, PARTS, ST], BF16)
        vst = sb("vst", [P, NT, H, VW])

        A = [bank("acc0"), bank("acc1")]
        TR = bank("turn")
        KQ = [bank("kq0"), bank("kq1")]
        NUM, DEN = bank("num"), bank("den_ps")
        U = bank("upd")

        w_ld = sem("w_ld")
        small_ld = sem("small_ld")
        x_ld = sem("x_ld")
        passed_sp, passed_v = sem("a_passed_sp"), sem("a_passed_v")
        made = sem("made")
        set_up = sem("set_up")
        var_ready = sem("var_ready")
        rstd_ready = sem("rstd_ready")
        norm_ready = sem("norm_ready")
        turned = sem("turned")
        turned_taken = sem("turned_taken")
        acc_full = sem("acc_full")
        exp_ready = sem("exp_ready")
        phi_ready = sem("phi_ready")
        acc_taken = sem("acc_taken")
        kq_full = sem("kq_full")
        masked = sem("masked")
        u_full = sem("u_full")
        u_taken = sem("u_taken")
        nd_full = sem("nd_full")
        nd_taken = sem("nd_taken")
        ffn_full = sem("ffn_full")
        ffn_taken = sem("ffn_taken")
        dve = sem("dve")
        stored = sem("stored")
        parts_ready = sem("parts_ready")
        x3_stored, qk_stored, v_stored = sem("x3_stored"), sem("qk_stored"), sem("v_stored")

        QK_USES, ACT_USES, U_USES = 2 * PAIRS, 2 * NT + FC + 2, 3 * NT + 1
        TURNS = DC + 2 * NT + DC + DC
        block = ctx.enter_context(nc.Block())

        def pairs_dram(t):
            return t.rearrange("(c p) n -> p c n", p=P)

        @block.sync
        def _(sp):
            from_one(sp, stored)
            xs = a["L0_attn_x"].rearrange("b (n p) d -> p (b n) d", p=P)
            sp.dma_start(x[:, 0:NT, :], xs[:, 0:NT, :]).then_inc(x_ld, 16)
            for dst, name in ((wk, "L0_attn_Wk"), (wq, "L0_attn_Wq"), (wv, "L0_attn_Wv"), (wo, "L0_attn_Wo"),
                              (wf1, "L0_attn_Wf1"), (wf2, "L0_attn_Wf2"), (kw, "L0_ffn_k_w"), (vw, "L0_ffn_v_w")):
                sp.dma_start(dst[:, :, :], pairs_dram(a[name])).then_inc(w_ld, 16)
            q_cols = pairs_dram(a["L0_ffn_q_w"]).rearrange("p c (h d) -> p c h d", h=H)
            for c in range(DC):
                sp.dma_start(qw[:, c, :].rearrange("p (h d) -> p h d", h=H), q_cols[:, c, :, 0:KPH]).then_inc(w_ld, 16)
            with sp.Fori(1, STEPS) as g:
                wait_apart(sp, x_ld, g * 16, passed_sp)
                sp.dma_start(x[:, bass.ds(g * NT, NT), :], xs[:, bass.ds(g * NT, NT), :]).then_inc(x_ld, 16)
            with sp.Fori(0, B) as b, sp.Fori(0, STEPS // B) as r:
                g = b * (STEPS // B) + r
                wait_apart(sp, parts_ready, 1 + g * 2 + 1, passed_sp)
                sp.dma_start(scratch["x3"][bass.ds(g, 1)].rearrange("g p n d -> p (g n) d"), x3[:, :, :]).then_inc(x3_stored, 16)
                sp.dma_start(scratch["v"][bass.ds(g, 1)].rearrange("g p n w -> p (g n) w"),
                             vst[:, :, :, :].rearrange("p n h w -> p n (h w)")).then_inc(v_stored, 16)
                wait_apart(sp, parts_ready, 1 + g * 2 + 2, passed_sp)
                for i in range(2):
                    sp.dma_start(scratch["qk"][i][:, bass.ds(b, 1), :, bass.ds(r * ST, ST)].rearrange("i b p s -> p (b i) s"),
                                 parts[:, i, :, :]).then_inc(qk_stored, 16)
                sp.wait_ge(x3_stored, g * 16 + 16)
                sp.wait_ge(v_stored, g * 16 + 16)
                sp.wait_ge(qk_stored, g * 32 + 32)
                sp.sem_inc(stored, 1)
            sp.wait_ge(x3_stored, 16 * STEPS)
            sp.wait_ge(v_stored, 16 * STEPS)
            sp.wait_ge(qk_stored, 32 * STEPS)

        SMALL = 16 * 7

        @block.gpsimd
        def _(pool):
            for dst, name in ((ln1g, "L0_attn_ln1_g"), (ln1b, "L0_attn_ln1_b"), (ln2g, "L0_attn_ln2_g"), (ln2b, "L0_attn_ln2_b")):
                pool.dma_start(dst[:, :], a[name].rearrange("(c p) -> p c", p=P),
                               allow_slow_non_contiguous=True).then_inc(small_ld, 16)
            pool.dma_start(qb[:, :], a["L0_ffn_q_b"].rearrange("(h e d) -> h e d", h=H, e=2)[:, 0, :]
                           .rearrange("h (d o) -> h d o", o=1), allow_slow_non_contiguous=True).then_inc(small_ld, 16)
            pool.dma_start(kb[:, :], a["L0_ffn_k_b"].rearrange("(p o) -> p o", o=1), allow_slow_non_contiguous=True).then_inc(small_ld, 16)
            pool.dma_start(vb[:, :], a["L0_ffn_v_b"].rearrange("(o n) -> o n", o=1).broadcast_to([P, LAT])).then_inc(small_ld, 16)
            identity_matrix(pool, ident[:, :], made)
            pool.memset(causal[:, :, :], 1.0).then_inc(made, 1)
            pool.wait_ge(made, 3)
            pool.affine_select(out=causal[:, :, :], in_=causal[:, :, :], compare_op=ALU.is_ge, fill=0.0, base=0,
                               pattern=[[0, 4], [1, P]], channel_multiplier=-1).then_inc(made, 1)
            pool.memset(minus_half[:, :], -0.5).then_inc(made, 1)
            pool.wait_ge(made, 5)
            with pool.Fori(0, STEPS) as g:
                for k in range(3):
                    pool.wait_ge(var_ready, g * 3 + k + 1)
                    pool.tensor_tensor(rstd[:, :], var_eps[:, :], minus_half[:, :], ALU.pow).then_inc(rstd_ready, 1)

        W_ALL = 16 * 10

        @block.vector
        def _(v):
            from_one(v, phi_ready, parts_ready, masked, u_taken, ffn_taken)
            v.memset(qT[:, :, :, :], 0.0).then_inc(set_up, 1)
            v.memset(state[:, :, :, :], 0.0).then_inc(set_up, 1)
            v.memset(vt[:, :, :, :], 1.0).then_inc(set_up, 1)
            v.memset(vst[:, :, :, :], 1.0).then_inc(set_up, 1)
            v.memset(ones[:, :], 1.0).then_inc(set_up, 1)
            v.memset(keep[:, :], 1.0).then_inc(set_up, 1)
            v.wait_ge(set_up, 6)
            for b in range(B):
                last = (b + 1) * (STEPS // B) - 1
                v.memset(keep[:, last:last + 1], 0.0).then_inc(set_up, 1)
            v.wait_ge(set_up, 8)
            v.wait_ge(made, 5)
            v.wait_ge(w_ld, W_ALL)
            v.wait_ge(small_ld, SMALL)

            with v.Fori(0, STEPS) as g:
                v.wait_ge(x_ld, g * 16 + 16)
                own = Steps(dve, 80)

                def step(instruction):
                    own.mark(instruction)
                    v.wait_ge(dve, own.value(g))

                def layer_norm(k, src, dst):
                    for t in range(NT):
                        own.mark(v.bn_stats(stats[:, t, :], src(t)))
                    wait_apart(v, dve, own.value(g), passed_v)
                    for t in range(NT):
                        own.mark(v.bn_aggr(meanvar[:, t, :], stats[:, t, :]))
                    v.wait_ge(dve, own.value(g))
                    v.tensor_scalar(var_eps[:, :], meanvar[:, :, 1], EPS_LN, None, ALU.add).then_inc(var_ready, 1)
                    v.wait_ge(rstd_ready, g * 3 + k + 1)
                    for t in range(NT):
                        v.tensor_scalar(dst[:, t, :], src(t), meanvar[:, t, 0:1], rstd[:, t:t + 1],
                                        ALU.subtract, ALU.mult).then_inc(norm_ready, 1)

                layer_norm(0, lambda t: x[:, bass.ds(g * NT + t, 1), :].rearrange("p a d -> p (a d)"), xn)

                for n in range(QK_USES):
                    pair = n % PAIRS
                    e = ex[:, n % 2, :]
                    v.wait_ge(exp_ready, g * QK_USES + n + 1)
                    step(v.tensor_scalar(e, e, 1.0, None, ALU.min))
                    if n < PAIRS:
                        v.scalar_tensor_tensor(kT[:, pair, :], A[n % 2][:, :], 0.0, e, ALU.max, ALU.add).then_inc(phi_ready, 1)
                    else:
                        own.mark(v.scalar_tensor_tensor(qT[0:DH, pair, 0, :], A[n % 2][0:DH, :], 0.0,
                                                        ex[0:DH, n % 2, :], ALU.max, ALU.add))
                        v.scalar_tensor_tensor(qT[DH:P, pair, 1, :], A[n % 2][DH:P, :], 0.0,
                                               ex[DH:P, n % 2, :], ALU.max, ALU.add).then_inc(phi_ready, 1)

                def mask(ch, q):
                    v.wait_ge(kq_full, g * 16 + 4 * ch + q + 1)
                    v.tensor_tensor(att[:, 4 * q:4 * q + 4, :], KQ[q % 2][:, :].rearrange("p (h s) -> p h s", h=4),
                                    causal[:, :, :], ALU.mult).then_inc(masked, 1)

                def update(ch, half, use):
                    v.wait_ge(u_full, g * U_USES + use + 1)
                    rows = slice(4 * half, 4 * half + 4)
                    v.tensor_tensor(state[:, (ch + 1) % 2, rows, :], U[:, :].rearrange("p (h w) -> p h w", h=4),
                                    state[:, ch % 2, rows, :], ALU.add).then_inc(u_taken, 1)

                def divide(ch, half):
                    v.wait_ge(nd_full, g * 8 + 2 * ch + half + 1)
                    step(v.tensor_scalar(den[:, :], DEN[:, :], EPS_DEN, None, ALU.max))
                    step(v.reciprocal(den[:, :], den[:, :]))
                    v.tensor_tensor(oT[:, 4 * half:4 * half + 4, :], NUM[:, :].rearrange("p (h s) -> p h s", h=4),
                                    den[:, :].rearrange("p (h s) -> p h s", h=4), ALU.mult).then_inc(nd_taken, 1)

                def residual(ch, use):
                    v.wait_ge(u_full, g * U_USES + use + 1)
                    v.tensor_tensor(x1[:, ch, :], U[:, 0:D], x[:, bass.ds(g * NT + ch, 1), :].rearrange("p a d -> p (a d)"),
                                    ALU.add).then_inc(u_taken, 1)

                for ch in range(NT):
                    mask(ch, 0)
                    mask(ch, 1)
                    update(ch, 0, 3 * ch - (ch > 0))
                    mask(ch, 2)
                    mask(ch, 3)
                    if ch:
                        residual(ch - 1, 3 * ch)
                    divide(ch, 0)
                    update(ch, 1, 3 * ch + 1)
                    divide(ch, 1)
                v.wait_ge(u_taken, 1 + g * U_USES + 11)
                step(v.tensor_scalar(state[:, 0, :, :], state[:, 0, :, :], keep[:, bass.ds(g, 1)], None, ALU.mult))
                residual(NT - 1, 3 * NT - 1)
                v.wait_ge(u_taken, 1 + g * U_USES + 12)

                layer_norm(1, lambda t: x1[:, t, :], xn)

                for t in range(NT):
                    v.wait_ge(ffn_full, g * NT + t + 1)
                    own.mark(v.tensor_tensor(y[:, t, :], [NUM, DEN][t % 2][:, 0:D], x1[:, t, :], ALU.add))
                    ffn_value = own.value(g)
                    v.wait_ge(dve, ffn_value)
                    v.tensor_tensor(y[:, t, :], y[:, t, :], x[:, bass.ds(g * NT + t, 1), :].rearrange("p a d -> p (a d)"),
                                    ALU.add).then_inc(ffn_taken, 1)
                v.wait_ge(ffn_taken, 1 + g * NT + NT)
                v.wait_ge(stored, 1 + g)
                layer_norm(2, lambda t: y[:, t, :], x3)

                v.wait_ge(u_full, g * U_USES + U_USES)
                for t in range(NT):
                    i = v.tensor_tensor(vst[:, t, :, 0:KPH], U[:, t * LAT:(t + 1) * LAT].rearrange("p (h d) -> p h d", h=H),
                                        vb[:, :].rearrange("p (h d) -> p h d", h=H), ALU.add)
                    if t < NT - 1:
                        own.mark(i)
                    else:
                        i.then_inc(u_taken, 1)
                v.wait_ge(dve, own.value(g))
                v.wait_ge(u_taken, 1 + g * U_USES + U_USES)
                v.wait_ge(norm_ready, g * 3 * NT + 3 * NT)
                v.sem_inc(parts_ready, 1)
                for i in range(2):
                    v.wait_ge(acc_taken, 1 + g * ACT_USES + ACT_USES - 1 + i)
                    step(v.tensor_copy(parts[:, i, 0, :], qk[:, i, :]))
                    step(v.tensor_tensor(rest[:, i, :], qk[:, i, :], parts[:, i, 0, :], ALU.subtract))
                    step(v.tensor_copy(parts[:, i, 1, :], rest[:, i, :]))
                    step(v.tensor_tensor(parts[:, i, 2, :], rest[:, i, :], parts[:, i, 1, :], ALU.subtract))
                v.sem_inc(parts_ready, 1)
                assert own.n == own.per, own.n

        @block.scalar
        def _(s):
            from_one(s, turned_taken, acc_taken)
            s.wait_ge(w_ld, W_ALL)
            s.wait_ge(small_ld, SMALL)
            s.wait_ge(set_up, 8)
            with s.Fori(0, STEPS) as g:
                def turn_affine(k, c, gain, shift):
                    s.wait_ge(turned, g * TURNS + k + 1)
                    s.activation(feat[:, c, :], TR[:, :], ACT.Identity, bias=shift, scale=gain).then_inc(turned_taken, 1)

                for c in range(DC):
                    turn_affine(c, c, ln1g[:, c:c + 1], ln1b[:, c:c + 1])
                for n in range(QK_USES):
                    s.wait_ge(acc_full, g * (QK_USES + ACT_USES) + n + 1)
                    s.wait_ge(phi_ready, 1 + g * QK_USES + max(n - 1, 0))
                    s.activation(ex[:, n % 2, :], A[n % 2][:, :], ACT.Exp).then_inc(exp_ready, 1)
                for ch in range(NT):
                    for half in range(2):
                        s.wait_ge(acc_full, g * (QK_USES + ACT_USES) + QK_USES + 2 * ch + half + 1)
                        s.activation(vt[:, 8 * half:8 * half + 8, 0, :], A[half][:, :].rearrange("p (h d) -> p h d", h=8),
                                     ACT.Copy).then_inc(acc_taken, 1)
                        s.wait_ge(turned, g * TURNS + DC + 2 * ch + half + 1)
                        s.activation(kt[:, 8 * half:8 * half + 8, :].rearrange("p h d -> p (h d)"), TR[:, :],
                                     ACT.Copy).then_inc(turned_taken, 1)
                for c in range(DC):
                    turn_affine(DC + 2 * NT + c, c, ln2g[:, c:c + 1], ln2b[:, c:c + 1])
                for j in range(FC):
                    s.wait_ge(acc_full, g * (QK_USES + ACT_USES) + QK_USES + 2 * NT + j + 1)
                    s.activation(fT[:, j, :], A[j % 2][:, :], ACT.Gelu).then_inc(acc_taken, 1)
                for c in range(DC):
                    s.wait_ge(turned, g * TURNS + 2 * DC + 2 * NT + c + 1)
                    s.activation(feat[:, c, :], TR[:, :], ACT.Copy).then_inc(turned_taken, 1)
                s.wait_ge(parts_ready, 1 + 2 * g)
                for i, bias in enumerate((qb, kb)):
                    s.wait_ge(acc_full, g * (QK_USES + ACT_USES) + QK_USES + 2 * NT + FC + i + 1)
                    s.activation(qk[:, i, :], A[i][:, :], ACT.Identity, bias=bias[:, :]).then_inc(acc_taken, 1)

        @block.tensor
        def _(pe):
            pe.wait_ge(w_ld, W_ALL)
            pe.wait_ge(set_up, 8)
            pe.wait_ge(made, 5)

            with pe.Fori(0, STEPS) as g:
                def turn(k, blocks, c=None):
                    pe.wait_ge(turned_taken, 1 + g * TURNS + k)
                    for i, block_in in enumerate(blocks):
                        if c is not None:
                            pe.wait_ge(norm_ready, g * 3 * NT + c * NT + i + 1)
                        last = pe.transpose(TR[:, i * P:(i + 1) * P], block_in, ident[:, :])
                    last.then_inc(turned, 1)

                def token_tiles(src, c):
                    return [src[:, t, c * P:(c + 1) * P] for t in range(NT)]

                def project(dst, lhs, rhs, full, chunks=DC):
                    for c in range(chunks):
                        last = pe.matmul(dst, lhs(c), rhs(c), start=(c == 0), stop=(c == chunks - 1))
                    last.then_inc(full, 1)

                for c in range(DC):
                    turn(c, token_tiles(xn, c), 0)
                pe.wait_ge(turned_taken, 1 + g * TURNS + DC)
                for n in range(QK_USES):
                    pair, w = n % PAIRS, (wk, wq)[n // PAIRS]
                    pe.wait_ge(acc_taken, 1 + g * ACT_USES)
                    if n >= 2:
                        pe.wait_ge(phi_ready, 1 + g * QK_USES + n - 1)
                    project(A[n % 2][:, :], lambda c: w[:, c, pair * P:(pair + 1) * P], lambda c: feat[:, c, :], acc_full)

                def values(ch, half):
                    if ch == 0:
                        pe.wait_ge(phi_ready, 1 + g * QK_USES + QK_USES - 1 + half)
                    else:
                        pe.wait_ge(acc_taken, 1 + g * ACT_USES + 2 * ch + half - 1)
                    project(A[half][:, :], lambda c: feat[:, c, ch * P:(ch + 1) * P],
                            lambda c: wv[:, c, half * 512:half * 512 + 512], acc_full)

                def turn_keys(ch, half):
                    turn(DC + 2 * ch + half, [kT[:, 4 * half + i, ch * P:(ch + 1) * P] for i in range(4)])

                def scores(ch, q):
                    pe.wait_ge(masked, 1 + g * 16 + max(4 * ch + q - 1, 0))
                    for i in range(2):
                        pair = 2 * q + i
                        last = pe.matmul(KQ[q % 2][:, i * 2 * P:(i + 1) * 2 * P].rearrange("p (h s) -> p h s", h=2),
                                         kT[:, pair, ch * P:(ch + 1) * P], qT[:, pair, :, ch * P:(ch + 1) * P],
                                         start=True, stop=True)
                    last.then_inc(kq_full, 1)

                def state_update(ch, half, use):
                    pe.wait_ge(u_taken, 1 + g * U_USES + use)
                    pe.wait_ge(turned_taken, 1 + g * TURNS + DC + 2 * ch + half + 1)
                    pe.wait_ge(acc_taken, 1 + g * ACT_USES + 2 * ch + half + 1)
                    for i in range(4):
                        for o in range(2):
                            h = 8 * half + 2 * i + o
                            last = pe.matmul(U[o * DH:(o + 1) * DH, i * P:(i + 1) * P], kt[:, h, :],
                                             vt[:, h, :, :].rearrange("p a d -> p (a d)"), start=True, stop=True)
                    last.then_inc(u_full, 1)

                def outputs(ch, half):
                    n = 2 * ch + half
                    if n == 0:
                        pe.wait_ge(ffn_taken, 1 + g * NT)
                    else:
                        pe.wait_ge(nd_taken, g * 8 + n)
                    pe.wait_ge(masked, 1 + g * 16 + 4 * ch + 2 * half + 2)
                    if n > 0:
                        pe.wait_ge(u_taken, 1 + g * U_USES + (3 * ch - 1 if half == 0 else 3 * ch + 1))
                    s0 = ch % 2
                    for i in range(4):
                        pair = 4 * half + i
                        cols = slice(i * P, (i + 1) * P)
                        for dst, lhs, w in ((NUM, lambda h: vt[:, h, 0, :], slice(0, DH)),
                                            (DEN, lambda h: ones[:, :], slice(DH, 2 * DH))):
                            for o in range(2):
                                pe.matmul(dst[o * DH:(o + 1) * DH, cols], lhs(2 * pair + o), att[:, 2 * pair + o, :],
                                          start=True, stop=False)
                            for o in range(2):
                                last = pe.matmul(dst[o * DH:(o + 1) * DH, cols], state[:, s0, pair, w],
                                                 qT[:, pair, o, ch * P:(ch + 1) * P], start=False, stop=True)
                    last.then_inc(nd_full, 1)

                def attention_out(ch, use):
                    pe.wait_ge(u_taken, 1 + g * U_USES + use)
                    pe.wait_ge(nd_taken, g * 8 + 2 * ch + 2)
                    project(U[:, 0:D], lambda c: oT[:, c, :], lambda c: wo[:, c, :], u_full, PAIRS)

                for ch in range(NT):
                    values(ch, 0)
                    turn_keys(ch, 0)
                    values(ch, 1)
                    scores(ch, 0)
                    turn_keys(ch, 1)
                    scores(ch, 1)
                    state_update(ch, 0, 3 * ch - (ch > 0))
                    scores(ch, 2)
                    scores(ch, 3)
                    if ch:
                        attention_out(ch - 1, 3 * ch)
                    outputs(ch, 0)
                    state_update(ch, 1, 3 * ch + 1)
                    outputs(ch, 1)
                attention_out(NT - 1, 3 * NT - 1)

                for c in range(DC):
                    turn(DC + 2 * NT + c, token_tiles(xn, c), 1)
                pe.wait_ge(turned_taken, 1 + g * TURNS + 2 * DC + 2 * NT)
                for j in range(FC):
                    pe.wait_ge(acc_taken, 1 + g * ACT_USES + 2 * NT + j - (j > 0))
                    project(A[j % 2][:, :], lambda c: wf1[:, c, j * P:(j + 1) * P], lambda c: feat[:, c, :], acc_full)
                for t in range(NT):
                    if t < 2:
                        pe.wait_ge(nd_taken, g * 8 + 8)
                    else:
                        pe.wait_ge(ffn_taken, 1 + g * NT + t - 1)
                    for j in range(FC):
                        if t == 0:
                            pe.wait_ge(acc_taken, 1 + g * ACT_USES + 2 * NT + j + 1)
                        last = pe.matmul([NUM, DEN][t % 2][:, 0:D], fT[:, j, t * P:(t + 1) * P], wf2[:, j, :],
                                         start=(j == 0), stop=(j == FC - 1))
                    last.then_inc(ffn_full, 1)

                for c in range(DC):
                    turn(2 * DC + 2 * NT + c, token_tiles(x3, c), 2)
                pe.wait_ge(turned_taken, 1 + g * TURNS + TURNS)
                pe.wait_ge(u_taken, 1 + g * U_USES + 3 * NT)
                for t in range(NT):
                    for c in range(DC):
                        last = pe.matmul(U[:, t * LAT:(t + 1) * LAT], feat[:, c, t * P:(t + 1) * P], vw[:, c, :],
                                         start=(c == 0), stop=(c == DC - 1))
                last.then_inc(u_full, 1)
                pe.wait_ge(acc_taken, 1 + g * ACT_USES + ACT_USES - 2)
                for i, w in enumerate((qw, kw)):
                    project(A[i][:, :], lambda c: w[:, c, :], lambda c: feat[:, c, :], acc_full)


GROUP = 4
GROUPS = B * H // GROUP
HEADS = B * H
TC = T // P
SB = T // 512
STACK = PARTS * PARTS * KPH
ROWS = 96
LEAD = TC + 4
VM = 32
STACK_DMAS = 2 * PARTS + 1


def softmax_attention_stage(nc, a, scratch, w1, w2, experts_ld):
    ctx = ExitStack()
    with ctx:
        def sb(name, shape, dt=F32):
            return ctx.enter_context(nc.sbuf_tensor(name, shape, dt))

        def ps(name, shape, dt=F32):
            return ctx.enter_context(nc.psum_tensor(name, shape, dt))

        def sem(name):
            return ctx.enter_context(nc.semaphore(name))

        qs = [sb(f"qs{i}", [P, T], BF16) for i in range(GROUP)]
        ks = [sb(f"ks{i}", [P, T], BF16) for i in range(GROUP)]
        zeros = sb("zeros", [P, T], BF16)
        identb = sb("identb", [P, P], BF16)
        v_in = sb("v_in", [P, STEPS, NT, H * VW])
        v_all = sb("v_all", [P, HEADS, TC, VW])
        vh = sb("vh", [P, 2, TC, VM])
        pt = sb("pt", [P, 2, T])
        tops = sb("tops", [P, TC, 2])
        top = sb("top", [P, TC])
        top_parts = sb("top_parts", [P, PARTS, TC], BF16)
        top_rows = sb("top_rows", [PARTS * TC, P], BF16)
        av_out = sb("av_out", [P, 2, 512])

        S1 = [ps(f"raw{i}", [P, 1024]) for i in range(2)]
        S2 = [ps(f"shifted{i}", [P, 512]) for i in range(2)]
        AV = ps("av", [P, 512])
        TR = ps("turned_tops", [PARTS * TC, P], BF16)

        stack_ld = [sem(f"stack_ld{i}") for i in range(GROUP)]
        shift_ld = [sem(f"shift_ld{i}") for i in range(GROUP)]
        v_ld, av_stored = sem("v_ld"), sem("av_stored")
        passed_sp, passed_pe = sem("b_passed_sp"), sem("b_passed_pe")
        b_made, padded = sem("b_made"), sem("padded")
        v_ready = sem("v_ready")
        v_head = sem("v_head")
        raw_full, raw_taken = sem("raw_full"), sem("raw_taken")
        tops_ready, tops_turned, rows_ready = sem("tops_ready"), sem("tops_turned"), sem("rows_ready")
        shifted_full, exp_done = sem("shifted_full"), sem("exp_done")
        av_tile = sem("av_tile")
        av_taken = sem("av_taken")
        av_free = sem("av_free")
        dve = sem("b_dve")
        block = ctx.enter_context(nc.Block())

        @block.sync
        def _(sp):
            sp.wait_ge(padded, 2 * GROUP - 1)
            sp.wait_ge(b_made, 6)

            def load_stacks(n, u):
                for i in range(PARTS):
                    r = i * PARTS * KPH
                    q_rows = scratch["qk"][0].rearrange("i b p s -> i (b p) s")[:, bass.ds(n * KPH, KPH), :]
                    k_rows = scratch["qk"][1, i:i + 1].rearrange("i b p s -> i (b p) s")[:, bass.ds(n * KPH, KPH), :]
                    sp.dma_start(qs[u][r:r + PARTS * KPH, :], q_rows).then_inc(stack_ld[u], 16)
                    sp.dma_start(ks[u][r:r + PARTS * KPH, :], k_rows.broadcast_to([PARTS, KPH, T])).then_inc(stack_ld[u], 16)
                sp.dma_start(qs[u][STACK:STACK + PARTS, :], zeros[0:PARTS, :]).then_inc(stack_ld[u], 16)

            def load_shift(n, u):
                wait_apart(sp, rows_ready, n + 1, passed_sp)
                sp.dma_start(qs[u][STACK:STACK + PARTS, :].rearrange("r (c s) -> r c s", c=TC), top_rows[:, :])\
                  .then_inc(shift_ld[u], 16)

            for u in range(GROUP):
                load_stacks(u, u)
            sp.dma_start(v_in[:, :, :, :], scratch["v"].rearrange("g p n w -> p g n w")).then_inc(v_ld, 16)
            load_shift(0, 0)
            for e in range(E):
                sp.dma_start(w1[:, e, :, :], a["L0_ffn_w1"][e].rearrange("(c p) n -> p c n", p=P)).then_inc(experts_ld, 16)
                sp.dma_start(w2[:, e, :, :], a["L0_ffn_w2"][e].rearrange("(c p) n -> p c n", p=P)).then_inc(experts_ld, 16)
            with sp.Fori(0, GROUPS - 1) as g:
                for u in range(GROUP):
                    n = g * GROUP + u
                    load_shift(n + 1, (u + 1) % GROUP)
                    wait_apart(sp, shifted_full, (n + 1) * (TC * SB), passed_sp)
                    load_stacks(n + GROUP, u)
            for u in range(GROUP - 1):
                load_shift(HEADS - GROUP + u + 1, u + 1)
            sp.wait_ge(experts_ld, 16 * 2 * E)

        @block.gpsimd
        def _(pool):
            pool.sem_inc(av_free, 2)
            pool.memset(identb[:, :], 0.0).then_inc(b_made, 1)
            pool.memset(zeros[:, :], 0.0).then_inc(b_made, 1)
            pool.wait_ge(b_made, 2)
            pool.affine_select(out=identb[:, :], in_=identb[:, :], compare_op=ALU.not_equal, fill=1.0, base=0,
                               pattern=[[-1, P]], channel_multiplier=1).then_inc(b_made, 1)
            first = STACK - 64
            pad = ks[0][64:ROWS, :]
            pool.wait_ge(b_made, 3)
            pool.memset(pad, -1.0).then_inc(b_made, 1)
            pool.wait_ge(b_made, 4)
            pool.affine_select(out=pad, in_=pad, compare_op=ALU.is_ge, fill=0.0, base=first + PARTS - 1,
                               pattern=[[0, T]], channel_multiplier=-1).then_inc(b_made, 1)
            pool.wait_ge(b_made, 5)
            pool.affine_select(out=pad, in_=pad, compare_op=ALU.is_ge, fill=0.0, base=-first,
                               pattern=[[0, T]], channel_multiplier=1).then_inc(b_made, 1)

            def head_values(n, u):
                pool.tensor_copy(vh[:, u, :, 0:VW], v_all[:, bass.ds(n, 1), :, :].rearrange("p o c w -> p (o c) w"))\
                    .then_inc(v_head, 1)

            def store(n, u):
                pool.wait_ge(av_taken, n + 1)
                for q in range(SB):
                    pool.dma_start(scratch["av"][bass.ds(n, 1), q].rearrange("o w s -> (o w) s"),
                                   av_out[q * VM:q * VM + VW, u, :]).then_inc(av_stored, 16)
                pool.wait_ge(av_stored, n * (16 * SB) + 16 * SB)
                pool.sem_inc(av_free, 1)

            pool.wait_ge(b_made, 6)
            pool.wait_ge(v_ready, 5)
            for u in range(2):
                head_values(u, u)
            with pool.Fori(0, HEADS // 2 - 1) as i:
                for u in range(2):
                    n = i * 2 + u
                    store(n, u)
                    pool.wait_ge(av_tile, 1 + (n + 1) * TC)
                    head_values(n + 2, u)
            for u in range(2):
                store(HEADS - 2 + u, u)
            pool.wait_ge(av_stored, 16 * SB * HEADS)

        @block.vector
        def _(v):
            v.memset(vh[:, :, :, :], 0.0).then_inc(v_ready, 1)
            v.wait_ge(b_made, 6)
            for u in range(GROUP):
                v.tensor_copy(qs[u][64:ROWS, :], zeros[64:ROWS, :]).then_inc(padded, 1)
                if u:
                    v.tensor_copy(ks[u][64:ROWS, :], ks[0][64:ROWS, :]).then_inc(padded, 1)

            def tile_maxima(n, c):
                for half in range(2):
                    v.wait_ge(raw_full, n * (2 * TC) + 2 * c + half + 1)
                    v.tensor_reduce(tops[:, c, half:half + 1], S1[half][:, :], axis=AX.X, op=ALU.max).then_inc(raw_taken, 1)

            def split_tops(n):
                v.wait_ge(raw_taken, (n + 1) * (2 * TC))
                v.tensor_tensor(top[:, :], tops[:, :, 0], tops[:, :, 1], ALU.max).then_inc(dve, 1)
                v.wait_ge(dve, n * 4 + 1)
                v.tensor_copy(top_parts[:, 0, :], top[:, :]).then_inc(dve, 1)
                for i in range(1, PARTS):
                    v.wait_ge(dve, n * 4 + 2 * i)
                    if i < PARTS - 1:
                        v.tensor_tensor(top[:, :], top[:, :], top_parts[:, i - 1, :], ALU.subtract).then_inc(dve, 1)
                        v.wait_ge(dve, n * 4 + 2 * i + 1)
                        v.tensor_copy(top_parts[:, i, :], top[:, :]).then_inc(dve, 1)
                    else:
                        v.tensor_tensor(top_parts[:, i, :], top[:, :], top_parts[:, i - 1, :], ALU.subtract).then_inc(tops_ready, 1)

            def take_rows(n):
                v.wait_ge(tops_turned, n + 1)
                v.tensor_copy(top_rows[:, :], TR[:, :]).then_inc(rows_ready, 1)

            def head(n, last):
                for c in range(2, TC):
                    tile_maxima(n, c)
                split_tops(n)
                if not last:
                    for c in range(2):
                        tile_maxima(n + 1, c)
                take_rows(n)

            for c in range(2):
                tile_maxima(0, c)
            with v.Fori(0, HEADS - 1) as n:
                head(n, False)
            head(HEADS - 1, True)

        @block.scalar
        def _(s):
            s.wait_ge(v_ld, 16)
            for b in range(B):
                tiles = v_in[:, b * (STEPS // B):(b + 1) * (STEPS // B), :, :].rearrange("p g n (h w) -> p (g n) h w", h=H)
                for part in range(2):
                    hs = slice(part * H // 2, (part + 1) * H // 2)
                    i = s.activation(v_all[:, b * H + hs.start:b * H + hs.stop, :, :].rearrange("p h c w -> p c h w"),
                                     tiles[:, :, hs, :], ACT.Copy)
                    i.then_inc(v_ready, 1)

            def exponentials(g, r):
                u, c = divmod(r, TC)
                n = g * GROUP + u
                for q in range(SB):
                    s.wait_ge(shifted_full, n * (TC * SB) + SB * c + q + 1)
                    if q == 0 and not (isinstance(g, int) and g == 0 and r < 2):
                        s.wait_ge(av_tile, 1 + n * TC + c - 1)
                    s.activation(pt[:, c % 2, q * 512:(q + 1) * 512], S2[q % 2][:, :], ACT.Exp, scale=KPH ** -0.5)\
                     .then_inc(exp_done, 1)
                    if q == 1 and c == 0 and r:
                        take_output(g, u - 1)

            def take_output(g, u):
                n = g * GROUP + u
                s.wait_ge(av_tile, 1 + (n + 1) * TC)
                s.wait_ge(av_free, n + 1)
                s.activation(av_out[:, u % 2, :], AV[:, :], ACT.Copy).then_inc(av_taken, 1)

            exponentials(0, 0)
            with s.Fori(0, GROUPS - 1) as g:
                for r in range(1, GROUP * TC + 1):
                    exponentials(g, r)
            for r in range(1, GROUP * TC):
                exponentials(GROUPS - 1, r)
            take_output(GROUPS - 1, GROUP - 1)

        @block.tensor
        def _(pe):
            from_one(pe, av_tile)
            pe.wait_ge(b_made, 6)

            def raw(g, r, k):
                u, c = divmod(r, TC)
                n = g * GROUP + u
                if isinstance(g, int) and n >= HEADS:
                    if n == HEADS and c == 1 and k == 0:
                        turn_tops(g, u - 1)
                    return
                if c == 1 and k == 0 and r > 1:
                    turn_tops(g, u - 1)
                if c == 0 and k == 0:
                    m = n // GROUP if isinstance(n, int) else g + u // GROUP
                    pe.wait_ge(stack_ld[u % GROUP], (m + 1) * (16 * STACK_DMAS))
                half, part = divmod(k, 2)
                if part == 0:
                    unit = 2 * c + half
                    if not (isinstance(n, int) and n == 0 and unit < 2):
                        pe.wait_ge(raw_taken, n * (2 * TC) + unit - 1)
                last = pe.matmul(S1[half][:, part * 512:(part + 1) * 512], qs[u % GROUP][0:ROWS, c * P:(c + 1) * P],
                                 ks[u % GROUP][0:ROWS, k * 512:(k + 1) * 512], start=True, stop=True)
                if part:
                    last.then_inc(raw_full, 1)

            def turn_tops(g, u):
                wait_apart(pe, tops_ready, g * GROUP + u + 1, passed_pe)
                pe.transpose(TR[:, :], top_parts[:, :, :].rearrange("p i c -> p (i c)"), identb[:, :]).then_inc(tops_turned, 1)

            def shifted(g, r, q):
                u, c = divmod(r, TC)
                n = g * GROUP + u
                if c == 0 and q == 0:
                    m = n // GROUP if isinstance(n, int) else g + u // GROUP
                    pe.wait_ge(shift_ld[u % GROUP], m * 16 + 16)
                if not (isinstance(n, int) and n == 0 and c == 0 and q < 2):
                    pe.wait_ge(exp_done, n * (TC * SB) + SB * c + q - 1)
                pe.matmul(S2[q % 2][:, :], ks[u % GROUP][0:ROWS, c * P:(c + 1) * P],
                          qs[u % GROUP][0:ROWS, q * 512:(q + 1) * 512], start=True, stop=True).then_inc(shifted_full, 1)

            def weigh(g, r):
                u, c = divmod(r, TC)
                n = g * GROUP + u
                if c == 0:
                    pe.wait_ge(v_head, n + 1)
                    if r:
                        pe.wait_ge(av_taken, n)
                pe.wait_ge(exp_done, n * (TC * SB) + SB * (c + 1))
                for q in range(SB):
                    last = pe.matmul(AV[q * VM:(q + 1) * VM, :], vh[:, u % 2, c, :], pt[:, c % 2, q * 512:(q + 1) * 512],
                                     start=(c == 0), stop=(c == TC - 1))
                last.then_inc(av_tile, 1)

            def tile_step(g, r):
                shifted(g, r, 0)
                raw(g, r + LEAD, 0)
                shifted(g, r, 1)
                raw(g, r + LEAD, 1)
                if r:
                    weigh(g, r - 1)
                shifted(g, r, 2)
                raw(g, r + LEAD, 2)
                shifted(g, r, 3)
                raw(g, r + LEAD, 3)

            for r in range(LEAD):
                for k in range(SB):
                    raw(0, r, k)
            tile_step(0, 0)
            with pe.Fori(0, GROUPS - 1) as g:
                for r in range(1, GROUP * TC + 1):
                    tile_step(g, r)
            for r in range(1, GROUP * TC):
                tile_step(GROUPS - 1, r)
            weigh(GROUPS - 1, GROUP * TC - 1)


def experts_stage(nc, a, scratch, w1, w2, out):
    ctx = ExitStack()
    with ctx:
        def sb(name, shape, dt=F32):
            return ctx.enter_context(nc.sbuf_tensor(name, shape, dt))

        def bank(name):
            return ctx.enter_context(nc.psum_tensor(name, [P, 512], F32))

        def sem(name):
            return ctx.enter_context(nc.semaphore(name))

        ow, rw = sb("ow", [P, D]), sb("rw", [P, DC, E])
        ob, b1 = sb("ob", [P, DC]), sb("b1", [P, E, EC])
        rb, b2 = sb("rb", [P, NT, E]), sb("b2", [E, D])
        ident = sb("c_ident", [P, P])
        iota_i, iota = sb("iota_i", [P, E], mybir.dt.int32), sb("iota", [P, E])
        minus_half = sb("c_minus_half", [P, NT])
        x3 = sb("c_x3", [P, STEPS * NT, D])
        num, den = sb("c_num", [LAT, ST]), sb("c_den", [LAT, ST])
        aoT = sb("aoT", [LAT, ST])
        mlaT = sb("mlaT", [P, DC, ST])
        logits = sb("logits", [P, NT, E])
        probs = sb("probs", [P, NT, E])
        small = sb("small", [P, NT])
        weight_sum = sb("weight_sum", [P, NT])
        best = sb("best", [P, NT, 8])
        best_at = sb("best_at", [P, NT, 8], U32)
        at_f = sb("at_f", [P, NT, 2])
        weight = sb("weight", [P, NT, 2])
        chosen = sb("chosen", [P, 2, NT, E])
        comb = sb("comb", [P, NT, E])
        combT = sb("combT", [E, ST])
        h1 = sb("h1", [P, 2, EC, ST])
        moe = sb("moe", [P, NT, D])
        stats = sb("c_stats", [P, NT, 6])
        meanvar = sb("c_meanvar", [P, NT, 2])
        var_eps, rstd = sb("c_var_eps", [P, NT]), sb("c_rstd", [P, NT])
        res = sb("res", [P, NT, D])

        A = [bank("h1_0"), bank("h1_1")]
        H2 = [bank(f"h2_{t}") for t in range(NT)]
        R, CT = bank("router"), bank("comb_ps")

        c_ld, c_small, ao_ld, x3_ld, out_stored = (sem(n) for n in ("c_ld", "c_small", "ao_ld", "x3_ld", "out_stored"))
        c_made = sem("c_made")
        res_free = sem("res_free")
        passed_sp, passed_v = sem("c_passed_sp"), sem("c_passed_v")
        ao_ready = sem("ao_ready")
        h1_full, h1_ready = sem("h1_full"), sem("h1_ready")
        h2_full, h2_taken = sem("h2_full"), sem("h2_taken")
        logits_full, logits_ready, exp_ready, comb_ready = (sem(n) for n in ("logits_full", "logits_ready", "c_exp", "comb_ready"))
        combT_full, combT_ready = sem("combT_full"), sem("combT_ready")
        var_ready, rstd_ready, res_ready = sem("c_var"), sem("c_rstd_ready"), sem("res_ready")
        dve = sem("c_dve")
        A_USES, H2_USES = DC + E * EC, (E + 1) * NT
        block = ctx.enter_context(nc.Block())

        @block.sync
        def _(sp):
            sp.dma_start(ow[:, :], a["L0_ffn_o_w"][0:LAT, :]).then_inc(c_ld, 16)
            sp.dma_start(rw[:, :, :], a["L0_ffn_router_w"].rearrange("(c p) e -> p c e", p=P)).then_inc(c_ld, 16)
            sp.dma_start(b2[:, :], a["L0_ffn_b2"]).then_inc(c_ld, 16)
            with sp.Fori(0, B) as b, sp.Fori(0, STEPS // B) as r:
                g = b * (STEPS // B) + r
                wait_apart(sp, ao_ready, 1 + g, passed_sp)
                heads = scratch["av"].rearrange("(b h) q w s -> b q h w s", b=B)[bass.ds(b, 1), bass.ds(r, 1)]\
                    .rearrange("b q h w s -> (b q h) w s")
                sp.dma_start(num[:, :], heads[:, 0:KPH, :]).then_inc(ao_ld, 16)
                sp.dma_start(den[:, :], heads[:, KPH:VW, :].broadcast_to([H, KPH, ST])).then_inc(ao_ld, 16)
                sp.dma_start(x3[:, bass.ds(g * NT, NT), :], scratch["x3"][bass.ds(g, 1)].rearrange("g p n d -> p (g n) d")).then_inc(x3_ld, 16)
                wait_apart(sp, x3_ld, g * 16 + 16, passed_sp)

        @block.gpsimd
        def _(pool):
            from_one(pool, res_free)
            pool.dma_start(ob[:, :], a["L0_ffn_o_b"].rearrange("(c p) -> p c", p=P),
                           allow_slow_non_contiguous=True).then_inc(c_small, 16)
            pool.dma_start(b1[:, :, :], a["L0_ffn_b1"].rearrange("e (j p) -> p e j", p=P),
                           allow_slow_non_contiguous=True).then_inc(c_small, 16)
            for t in range(NT):
                pool.dma_start(rb[:, t, :], a["L0_ffn_router_b"].rearrange("(o n) -> o n", o=1).broadcast_to([P, E])).then_inc(c_small, 16)
            identity_matrix(pool, ident[:, :], c_made)
            pool.iota(iota_i[:, :], pattern=[[1, E]], base=0, channel_multiplier=0).then_inc(c_made, 1)
            pool.memset(minus_half[:, :], -0.5).then_inc(c_made, 1)
            pool.wait_ge(c_made, 4)
            outs = out.rearrange("b (n p) d -> p (b n) d", p=P)
            with pool.Fori(0, STEPS) as g:
                pool.wait_ge(var_ready, g + 1)
                pool.tensor_tensor(rstd[:, :], var_eps[:, :], minus_half[:, :], ALU.pow).then_inc(rstd_ready, 1)
                pool.wait_ge(res_ready, g * NT + NT)
                pool.dma_start(outs[:, bass.ds(g * NT, NT), :], res[:, :, :]).then_inc(out_stored, 16)
                pool.wait_ge(out_stored, g * 16 + 16)
                pool.sem_inc(res_free, 1)
            pool.wait_ge(out_stored, 16 * STEPS)

        @block.vector
        def _(v):
            from_one(v, ao_ready, h2_taken)
            v.wait_ge(c_small, 16 * (2 + NT))
            v.wait_ge(c_made, 4)
            v.tensor_copy(iota[:, :], iota_i[:, :]).then_inc(c_made, 1)
            v.wait_ge(c_made, 5)

            def attention_out(g, value):
                v.wait_ge(ao_ld, g * 32 + 32)
                v.reciprocal(den[:, :], den[:, :]).then_inc(dve, 1)
                v.wait_ge(dve, value)
                v.tensor_tensor(aoT[:, :], num[:, :], den[:, :], ALU.mult).then_inc(ao_ready, 1)

            def body(g, last):
                own = Steps(dve, 44)

                def value():
                    return own.value(g) + 1

                def step(instruction):
                    own.mark(instruction)
                    v.wait_ge(dve, value())

                def by_expert(column):
                    return column.rearrange("p (t o) -> p t o", o=1).broadcast_to([P, NT, E])

                v.wait_ge(logits_full, g + 1)
                step(v.tensor_tensor(logits[:, :, :], R[:, 0:NT * E].rearrange("p (t e) -> p t e", t=NT), rb[:, :, :], ALU.add))
                step(v.tensor_reduce(small[:, :], logits[:, :, :], axis=AX.X, op=ALU.max))
                v.tensor_tensor(logits[:, :, :], logits[:, :, :], by_expert(small[:, :]), ALU.subtract).then_inc(logits_ready, 1)
                v.wait_ge(exp_ready, g + 1)
                step(v.tensor_reduce(small[:, :], probs[:, :, :], axis=AX.X, op=ALU.add))
                step(v.reciprocal(small[:, :], small[:, :]))
                own.mark(v.tensor_tensor(probs[:, :, :], probs[:, :, :], by_expert(small[:, :]), ALU.mult))
                wait_apart(v, dve, value(), passed_v)
                for t in range(NT):
                    own.mark(v.max(best[:, t, :], probs[:, t, :]))
                wait_apart(v, dve, value(), passed_v)
                for t in range(NT):
                    own.mark(v.max_index(best_at[:, t, :], best[:, t, :], probs[:, t, :]))
                step(v.tensor_tensor(weight_sum[:, :], best[:, :, 0], best[:, :, 1], ALU.add))
                step(v.tensor_scalar(weight_sum[:, :], weight_sum[:, :], 1e-8, None, ALU.add))
                own.mark(v.tensor_copy(at_f[:, :, :], best_at[:, :, 0:2]))
                step(v.reciprocal(weight_sum[:, :], weight_sum[:, :]))
                for k in range(2):
                    own.mark(v.tensor_tensor(weight[:, :, k], best[:, :, k], weight_sum[:, :], ALU.mult))
                v.wait_ge(dve, value())
                for t in range(NT):
                    for k in range(2):
                        own.mark(v.tensor_scalar(chosen[:, k, t, :], iota[:, :], at_f[:, t, k:k + 1], weight[:, t, k:k + 1],
                                                 ALU.is_equal, ALU.mult))
                v.wait_ge(dve, value())
                v.tensor_tensor(comb[:, :, :], chosen[:, 0, :, :], chosen[:, 1, :, :], ALU.add).then_inc(comb_ready, 1)
                v.wait_ge(combT_full, g + 1)
                v.tensor_copy(combT[:, :], CT[0:E, :]).then_inc(combT_ready, 1)

                for t in range(NT):
                    v.wait_ge(h2_full, g * H2_USES + t + 1)
                    v.tensor_copy(moe[:, t, :], H2[t][:, 0:D]).then_inc(h2_taken, 1)
                for e in range(E):
                    for t in range(NT):
                        use = (e + 1) * NT + t
                        v.wait_ge(h2_full, g * H2_USES + use + 1)
                        v.wait_ge(h2_taken, 1 + g * H2_USES + use + 1 - NT)
                        v.scalar_tensor_tensor(moe[:, t, :], H2[t][:, 0:D], comb[:, t, e:e + 1], moe[:, t, :],
                                               ALU.mult, ALU.add).then_inc(h2_taken, 1)
                    if e == E - 3 and not last:
                        attention_out(g + 1, value() + 1)
                        own.n += 1
                v.wait_ge(h2_taken, 1 + (g + 1) * H2_USES)

                v.wait_ge(x3_ld, g * 16 + 16)
                for k in range(2):
                    for t in range(NT):
                        tile = x3[:, bass.ds(g * NT + t, 1), :].rearrange("p a d -> p (a d)")
                        if k == 0:
                            own.mark(v.scalar_tensor_tensor(moe[:, t, :], moe[:, t, :], 0.3, tile, ALU.mult, ALU.add))
                        else:
                            own.mark(v.tensor_tensor(moe[:, t, :], moe[:, t, :], tile, ALU.add))
                    v.wait_ge(dve, value())
                for t in range(NT):
                    own.mark(v.bn_stats(stats[:, t, :], moe[:, t, :]))
                wait_apart(v, dve, value(), passed_v)
                for t in range(NT):
                    own.mark(v.bn_aggr(meanvar[:, t, :], stats[:, t, :]))
                v.wait_ge(dve, value())
                v.tensor_scalar(var_eps[:, :], meanvar[:, :, 1], EPS_LN, None, ALU.add).then_inc(var_ready, 1)
                v.wait_ge(rstd_ready, g + 1)
                v.wait_ge(res_free, 1 + g)
                for t in range(NT):
                    v.tensor_scalar(res[:, t, :], moe[:, t, :], meanvar[:, t, 0:1], rstd[:, t:t + 1],
                                    ALU.subtract, ALU.mult).then_inc(res_ready, 1)
                assert last or own.n == own.per, own.n

            attention_out(0, 1)
            with v.Fori(0, STEPS - 1) as g:
                body(g, False)
            body(STEPS - 1, True)

        @block.scalar
        def _(s):
            s.wait_ge(c_small, 16 * (2 + NT))

            def project_out(g):
                for c in range(DC):
                    s.wait_ge(h1_full, g * A_USES + c + 1)
                    s.activation(mlaT[:, c, :], A[c][:, :], ACT.Identity, bias=ob[:, c:c + 1]).then_inc(h1_ready, 1)
                s.wait_ge(logits_ready, g + 1)
                s.activation(probs[:, :, :], logits[:, :, :], ACT.Exp).then_inc(exp_ready, 1)

            def hidden(g, e):
                for j in range(EC):
                    use = DC + e * EC + j
                    s.wait_ge(h1_full, g * A_USES + use + 1)
                    s.activation(h1[:, e % 2, j, :], A[j % 2][:, :], ACT.Gelu, bias=b1[:, e, j:j + 1]).then_inc(h1_ready, 1)

            def body(g, last):
                for e in range(E):
                    hidden(g, e)
                if not last:
                    project_out(g + 1)

            project_out(0)
            with s.Fori(0, STEPS - 1) as g:
                body(g, False)
            body(STEPS - 1, True)

        @block.tensor
        def _(pe):
            pe.wait_ge(c_ld, 16 * 3)
            pe.wait_ge(c_made, 4)

            def free_h1(g, use):
                n = g * A_USES + use - 1
                if not isinstance(g, int) or n > 0:
                    pe.wait_ge(h1_ready, n)

            def front(g):
                pe.wait_ge(ao_ready, 1 + g + 1)
                for c in range(DC):
                    free_h1(g, c)
                    pe.matmul(A[c][:, :], ow[:, c * P:(c + 1) * P], aoT[:, :], start=True, stop=True).then_inc(h1_full, 1)
                pe.wait_ge(h1_ready, g * A_USES + DC)
                if not isinstance(g, int):
                    pe.wait_ge(logits_ready, g)
                for t in range(NT):
                    for c in range(DC):
                        last = pe.matmul(R[:, t * E:(t + 1) * E], mlaT[:, c, t * P:(t + 1) * P], rw[:, c, :],
                                         start=(c == 0), stop=(c == DC - 1))
                last.then_inc(logits_full, 1)

            def hidden(g, e):
                for j in range(EC):
                    free_h1(g, DC + e * EC + j)
                    for c in range(DC):
                        last = pe.matmul(A[j % 2][:, :], w1[:, e, c, j * P:(j + 1) * P], mlaT[:, c, :],
                                         start=(c == 0), stop=(c == DC - 1))
                    last.then_inc(h1_full, 1)

            def free_h2(g, use):
                n = g * H2_USES + use - NT + 1
                if not isinstance(g, int):
                    pe.wait_ge(h2_taken, 1 + g * H2_USES + max(use - NT + 1, 0))
                elif n > 0:
                    pe.wait_ge(h2_taken, 1 + n)

            def second_biases(g):
                pe.wait_ge(comb_ready, g + 1)
                for t in range(NT):
                    last = pe.transpose(CT[0:E, t * P:(t + 1) * P], comb[:, t, :], ident[:, :])
                last.then_inc(combT_full, 1)
                pe.wait_ge(combT_ready, g + 1)
                for t in range(NT):
                    free_h2(g, t)
                    pe.matmul(H2[t][:, 0:D], combT[:, t * P:(t + 1) * P], b2[:, :], start=True, stop=True).then_inc(h2_full, 1)

            def expert_out(g, e):
                pe.wait_ge(h1_ready, g * A_USES + DC + (e + 1) * EC)
                for t in range(NT):
                    free_h2(g, (e + 1) * NT + t)
                    for j in range(EC):
                        last = pe.matmul(H2[t][:, 0:D], h1[:, e % 2, j, t * P:(t + 1) * P], w2[:, e, j, :],
                                         start=(j == 0), stop=(j == EC - 1))
                    last.then_inc(h2_full, 1)

            def body(g, last):
                hidden(g, 0)
                hidden(g, 1)
                second_biases(g)
                for e in range(2, E):
                    expert_out(g, e - 2)
                    hidden(g, e)
                expert_out(g, E - 2)
                if not last:
                    front(g + 1)
                expert_out(g, E - 1)

            front(0)
            with pe.Fori(0, STEPS - 1) as g:
                body(g, False)
            body(STEPS - 1, True)


def post_ln_block(nc, a, out):
    def dram(name, shape, dt=F32):
        return nc.dram_tensor(name, shape, dt).ap()

    scratch = {
        "x3": dram("x3_scratch", [STEPS, P, NT, D]),
        "v": dram("v_scratch", [STEPS, P, NT, H * VW]),
        "qk": dram("qk_scratch", [2, PARTS, B, LAT, T], BF16),
        "av": dram("av_scratch", [HEADS, SB, VW, 512]),
    }
    linear_attention_stage(nc, a, scratch)
    with (
        nc.sbuf_tensor("w1", [P, E, DC, EF], F32) as w1,
        nc.sbuf_tensor("w2", [P, E, EC, D], F32) as w2,
        nc.semaphore("experts_ld") as experts_ld,
    ):
        softmax_attention_stage(nc, a, scratch, w1, w2, experts_ld)
        experts_stage(nc, a, scratch, w1, w2, out)


_IN = ["L0_attn_" + n for n in ("x", "ln1_g", "ln1_b", "Wq", "Wk", "Wv", "Wo", "ln2_g", "ln2_b", "Wf1", "Wf2")] + \
      ["L0_ffn_" + n for n in ("q_w", "q_b", "k_w", "k_b", "v_w", "v_b", "o_w", "o_b", "router_w", "router_b",
                               "w1", "b1", "w2", "b2")]


def kernel(**inputs):
    import numpy as np
    import concourse.bacc as bacc
    from concourse.bass_utils import run_bass_kernel_spmd

    nc = bacc.Bacc("TRN2", target_bir_lowering=False, num_devices=1)
    arrays, aps = {}, {}
    for name in _IN:
        arrays[f"in_{name}"] = np.ascontiguousarray(inputs[name])
        aps[name] = nc.dram_tensor(f"in_{name}", arrays[f"in_{name}"].shape, F32, kind="ExternalInput").ap()
    out = nc.dram_tensor("out", [B, T, D], F32, kind="ExternalOutput").ap()
    post_ln_block(nc, aps, out)
    r = run_bass_kernel_spmd(nc, [arrays], core_ids=[0])
    return r.results[0]["out"]
```

```python
from contextlib import ExitStack

import concourse.bass as bass
from concourse import mybir

F32 = mybir.dt.float32
BF16 = mybir.dt.bfloat16
U32 = mybir.dt.uint32
F32R = mybir.dt.float32r
ACT = mybir.ActivationFunctionType
ALU = mybir.AluOpType
AX = mybir.AxisListType

P = 128
B, T, D = 2, 2048, 256
N = B * T
ST = 512
NT = ST // P
STEPS = N // ST
DC = D // P
H = 16
DH = 64
PAIRS = H // 2
DF = 1024
FC = DF // P
LAT = D // 2
KPH = LAT // H
VW = KPH + 1
PARTS = 3
E = 8
EF = 2 * D
EC = EF // P
EPS_LN = 1e-5
EPS_DEN = 1e-6


def identity_matrix(eng, tile, done):
    eng.memset(tile, 0.0).then_inc(done, 1)
    eng.wait_ge(done, 1)
    eng.affine_select(out=tile, in_=tile, compare_op=ALU.not_equal, fill=1.0, base=0,
                      pattern=[[-1, P]], channel_multiplier=1).then_inc(done, 1)


def from_one(eng, *sems):
    for sem in sems:
        eng.sem_inc(sem, 1)


def wait_apart(eng, sem, value, passed):
    eng.wait_ge(sem, value)
    eng.sem_inc(passed, 1)


class Steps:

    def __init__(self, sem, per):
        self.sem, self.per, self.n = sem, per, 0

    def mark(self, instruction):
        self.n += 1
        instruction.then_inc(self.sem, 1)

    def value(self, g):
        return g * self.per + self.n


def linear_attention_stage(nc, a, scratch):
    ctx = ExitStack()
    with ctx:
        def sb(name, shape, dt=F32):
            return ctx.enter_context(nc.sbuf_tensor(name, shape, dt))

        def bank(name):
            return ctx.enter_context(nc.psum_tensor(name, [P, 512], F32))

        def sem(name):
            return ctx.enter_context(nc.semaphore(name))

        wk, wq = (sb(n, [P, 2, DC, H * DH], F32R) for n in ("wk", "wq"))
        wv = sb("wv", [P, DC, H * DH])
        wo = sb("wo", [P, PAIRS, D])
        wf1 = sb("wf1", [P, DC, DF])
        wf2 = sb("wf2", [P, FC, D])
        qw, kw, vw = (sb(n, [P, DC, LAT]) for n in ("qw", "kw", "vw"))
        ln1g, ln1b, ln2g, ln2b = (sb(n, [P, DC]) for n in ("ln1g", "ln1b", "ln2g", "ln2b"))
        qb, kb = sb("qb", [LAT, 1]), sb("kb", [LAT, 1])
        vb = sb("vb", [P, LAT])
        ident = sb("ident", [P, P])
        causal = sb("causal", [P, 4, P])
        keep = sb("keep", [P, STEPS])
        ones = sb("ones", [P, DH])
        minus_half = sb("minus_half", [P, NT])
        x_norm = sb("x_norm", [P, NT, D])
        x = sb("x", [P, NT, D])
        xn = sb("xn", [P, NT, D])
        feat = sb("feat", [P, DC, ST])
        feat_parts = sb("feat_parts", [P, 2, DC, ST], F32R)
        feat2 = sb("feat2", [P, DC, ST])
        stats = sb("stats", [P, NT, 6])
        meanvar = sb("meanvar", [P, NT, 2])
        var_eps = sb("var_eps", [P, NT])
        rstd = sb("rstd", [P, NT])
        ex = sb("ex", [P, 2, ST])
        qT = sb("qT", [P, PAIRS, 2, ST])
        kT = sb("kT", [P, PAIRS, ST])
        fT = sb("fT", [P, FC, ST])
        att = fT[:, 0:4, :].rearrange("p f (h s) -> p (f h) s", s=P)
        kt = fT[:, 4:6, :].rearrange("p f (h d) -> p (f h) d", d=DH)
        oT = fT[:, 6:8, :].rearrange("p f (h s) -> p (f h) s", s=P)
        vt = sb("vt", [P, H, 2, DH])
        den = sb("den", [P, ST])
        state = sb("state", [P, 2, PAIRS, 2 * DH])
        x1 = sb("x1", [P, NT, D])
        y = x1
        x3 = sb("x3", [P, NT, D])
        qk = sb("qk", [P, 2, ST])
        rest = sb("rest", [P, ST])
        parts = sb("parts", [P, 2, PARTS, ST], BF16)
        vst = sb("vst", [P, NT, H, VW])

        A = [bank("acc0"), bank("acc1")]
        TR = bank("turn")
        KQ = [bank("kq0"), bank("kq1")]
        Z = A + KQ
        V2 = KQ[1]
        NUM, DEN = bank("num"), bank("den_ps")
        U = bank("upd")
        TURNED = [[TR, TR], [TR, DEN], [TR, TR]]

        w_ld = sem("w_ld")
        in_ld = [sem("wk_ld"), sem("wq_ld")]
        in_split = [sem("wk_split"), sem("wq_split")]
        feat_split = sem("feat_split")
        small_ld = sem("small_ld")
        x_ld, x_norm_ld, x_first_ld = sem("x_ld"), sem("x_norm_ld"), sem("x_first_ld")
        passed_sp, passed_v = sem("a_passed_sp"), sem("a_passed_v")
        passed_pool = sem("a_passed_pool")
        made = sem("made")
        set_up = sem("set_up")
        qT_clear = sem("qT_clear")
        var_ready, rstd_ready, norm_ready, norm_turned, norm_taken = (
            [sem(f"{n}{k + 1}") for k in range(3)] for n in ("var_ready", "rstd_ready", "norm_ready", "norm_turned", "norm_taken"))
        keys_turned, keys_taken = sem("keys_turned"), sem("keys_taken")
        k_full, k_exp, k_phi = sem("k_full"), sem("k_exp"), sem("k_phi")
        q_full, q_exp, q_phi = sem("q_full"), sem("q_exp"), sem("q_phi")
        below_ready = sem("below_ready")
        v_full, v_taken = sem("v_full"), sem("v_taken")
        kq_full, masked = sem("kq_full"), sem("masked")
        u_full, u_taken = sem("u_full"), sem("u_taken")
        nd_full = sem("nd_full")
        num_taken, den_taken = sem("num_taken"), sem("den_taken")
        o_ready = sem("o_ready")
        hidden_full, hidden_ready = sem("hidden_full"), sem("hidden_ready")
        ffn_full, ffn_taken = sem("ffn_full"), sem("ffn_taken")
        v2_full, v2_taken = sem("v2_full"), sem("v2_taken")
        qk_full, qk_taken = sem("qk_full"), sem("qk_taken")
        dve = sem("dve")
        parts_ready = sem("parts_ready")
        x3_free, parts_free = sem("x3_free"), sem("parts_free")
        x3_stored, qk_stored, v_stored = sem("x3_stored"), sem("qk_stored"), sem("v_stored")
        U_USES = 3 * NT
        SMALL = 16 * 7
        K_EARLY = PAIRS - 2
        block = ctx.enter_context(nc.Block())

        def by_chunk(t):
            return t.rearrange("(c p) n -> p c n", p=P)

        def w_staged(i):
            return qT[:, 2 * i:2 * i + 2, :, :].rearrange("p c o s -> p c (o s)")

        xs = a["L0_attn_x"].rearrange("b (n p) d -> p (b n) d", p=P)

        @block.sync
        def _(sp):
            from_one(sp, x3_free, parts_free)
            sp.dma_start(x_norm[:, :, :], xs[:, 0:NT, :]).then_inc(x_first_ld, 16)
            for i, name in enumerate(("L0_attn_Wk", "L0_attn_Wq")):
                sp.dma_start(w_staged(i), by_chunk(a[name])).then_inc(in_ld[i], 16)
            sp.wait_ge(small_ld, SMALL)
            for dst, name in ((wv, "L0_attn_Wv"), (wo, "L0_attn_Wo"),
                              (wf1, "L0_attn_Wf1"), (wf2, "L0_attn_Wf2"), (kw, "L0_ffn_k_w"), (vw, "L0_ffn_v_w")):
                sp.dma_start(dst[:, :, :], by_chunk(a[name])).then_inc(w_ld, 16)
            q_cols = by_chunk(a["L0_ffn_q_w"]).rearrange("p c (h d) -> p c h d", h=H)
            for c in range(DC):
                sp.dma_start(qw[:, c, :].rearrange("p (h d) -> p h d", h=H), q_cols[:, c, :, 0:KPH]).then_inc(w_ld, 16)
            with sp.Fori(0, B) as b, sp.Fori(0, STEPS // B) as r:
                g = b * (STEPS // B) + r
                wait_apart(sp, norm_ready[2], g * NT + NT, passed_sp)
                sp.dma_start(scratch["x3"][bass.ds(g, 1)].rearrange("g p n d -> p (g n) d"), x3[:, :, :]).then_inc(x3_stored, 16)
                sp.wait_ge(x3_stored, g * 16 + 16)
                sp.sem_inc(x3_free, 1)
                wait_apart(sp, v2_taken, g * NT + NT, passed_sp)
                sp.dma_start(scratch["v"].rearrange("p t (b w) -> p t b w", b=B)[:, bass.ds(r * NT, NT), bass.ds(b, 1), :]
                             .rearrange("p t b w -> p t (b w)"),
                             vst[:, :, :, :].rearrange("p n h w -> p n (h w)")).then_inc(v_stored, 16)
                wait_apart(sp, parts_ready, g * 2 + 2, passed_sp)
                for i in range(2):
                    sp.dma_start(scratch["qk"][i][:, bass.ds(b, 1), :, bass.ds(r * ST, ST)].rearrange("i b p s -> p (b i) s"),
                                 parts[:, i, :, :]).then_inc(qk_stored, 16)
                sp.wait_ge(v_stored, g * 16 + 16)
                sp.wait_ge(qk_stored, g * 32 + 32)
                sp.sem_inc(parts_free, 1)
            sp.wait_ge(x3_stored, 16 * STEPS)
            sp.wait_ge(v_stored, 16 * STEPS)
            sp.wait_ge(qk_stored, 32 * STEPS)

        @block.gpsimd
        def _(pool):
            for dst, name in ((ln1g, "L0_attn_ln1_g"), (ln1b, "L0_attn_ln1_b"), (ln2g, "L0_attn_ln2_g"), (ln2b, "L0_attn_ln2_b")):
                pool.dma_start(dst[:, :], a[name].rearrange("(c p) -> p c", p=P),
                               allow_slow_non_contiguous=True).then_inc(small_ld, 16)
            pool.dma_start(qb[:, :], a["L0_ffn_q_b"].rearrange("(h e d) -> h e d", h=H, e=2)[:, 0, :]
                           .rearrange("h (d o) -> h d o", o=1), allow_slow_non_contiguous=True).then_inc(small_ld, 16)
            pool.dma_start(kb[:, :], a["L0_ffn_k_b"].rearrange("(p o) -> p o", o=1), allow_slow_non_contiguous=True).then_inc(small_ld, 16)
            pool.dma_start(vb[:, :], a["L0_ffn_v_b"].rearrange("(o n) -> o n", o=1).broadcast_to([P, LAT])).then_inc(small_ld, 16)
            pool.memset(minus_half[:, :], -0.5).then_inc(made, 1)
            pool.wait_ge(made, 1)
            pool.memset(ident[:, :], 0.0).then_inc(made, 1)
            pool.wait_ge(made, 2)
            pool.affine_select(out=ident[:, :], in_=ident[:, :], compare_op=ALU.not_equal, fill=1.0, base=0,
                               pattern=[[-1, P]], channel_multiplier=1).then_inc(made, 1)
            pool.memset(causal[:, :, :], 1.0).then_inc(made, 1)
            pool.wait_ge(made, 4)
            pool.affine_select(out=causal[:, :, :], in_=causal[:, :, :], compare_op=ALU.is_ge, fill=0.0, base=0,
                               pattern=[[0, 4], [1, P]], channel_multiplier=-1).then_inc(made, 1)
            pool.wait_ge(made, 5)

            def root(k, g):
                pool.wait_ge(var_ready[k], g + 1)
                pool.tensor_tensor(rstd[:, :], var_eps[:, :], minus_half[:, :], ALU.pow).then_inc(rstd_ready[k], 1)

            def load_x_norm(g):
                wait_apart(pool, norm_ready[0], g * NT, passed_pool)
                pool.dma_start(x_norm[:, :, :], xs[:, bass.ds(g * NT, NT), :]).then_inc(x_norm_ld, 16)

            def body(g, first, last):
                if not first:
                    wait_apart(pool, ffn_taken, g * NT, passed_pool)
                pool.dma_start(x[:, :, :], xs[:, bass.ds(g * NT, NT), :]).then_inc(x_ld, 16)
                if not last:
                    load_x_norm(g + 1)
                if not first:
                    root(2, g - 1)
                if not last:
                    root(0, g + 1)
                root(1, g)

            root(0, 0)
            pool.wait_ge(in_split[0], 8)
            pool.wait_ge(in_split[1], 8)
            pool.memset(qT[:, :, :, :], 0.0).then_inc(qT_clear, 1)
            body(0, True, False)
            with pool.Fori(1, STEPS - 1) as g:
                body(g, False, False)
            body(STEPS - 1, False, True)
            root(2, STEPS - 1)

        W_ALL = 16 * 8

        @block.vector
        def _(v):
            v.memset(keep[:, :], 1.0).then_inc(set_up, 1)
            v.memset(ones[:, :], 1.0).then_inc(set_up, 1)
            v.wait_ge(set_up, 1)
            for b in range(B):
                last_step = (b + 1) * (STEPS // B) - 1
                v.memset(keep[:, last_step:last_step + 1], 0.0).then_inc(set_up, 1)

            own = Steps(dve, 45)

            def split_input(i):
                w = (wk, wq)[i]
                v.wait_ge(in_ld[i], 16)
                for c in range(DC):
                    for cols in (slice(0, 512), slice(512, 1024)):
                        v.tensor_copy(w[:, 0, c, cols], w_staged(i)[:, c, cols]).then_inc(in_split[i], 1)
                v.wait_ge(in_split[i], 4)
                for c in range(DC):
                    for cols in (slice(0, 512), slice(512, 1024)):
                        v.tensor_tensor(w[:, 1, c, cols], w_staged(i)[:, c, cols], w[:, 0, c, cols],
                                        ALU.subtract).then_inc(in_split[i], 1)

            def split_feat(g, c, base):
                v.wait_ge(norm_taken[0], g * DC + c + 1)
                own.mark(v.tensor_copy(feat_parts[:, 0, c, :], feat[:, c, :]))
                v.wait_ge(dve, own.value(base))
                v.tensor_tensor(feat_parts[:, 1, c, :], feat[:, c, :], feat_parts[:, 0, c, :], ALU.subtract).then_inc(feat_split, 1)

            def statistics(k, g, base, src):
                for t in range(NT):
                    own.mark(v.bn_stats(stats[:, t, :], src(t)))
                wait_apart(v, dve, own.value(base), passed_v)
                for t in range(NT):
                    own.mark(v.bn_aggr(meanvar[:, t, :], stats[:, t, :]))
                v.wait_ge(dve, own.value(base))
                v.tensor_scalar(var_eps[:, :], meanvar[:, :, 1], EPS_LN, None, ALU.add).then_inc(var_ready[k], 1)

            def normalise(k, g, src, dst):
                v.wait_ge(rstd_ready[k], g + 1)
                for t in range(NT):
                    v.tensor_scalar(dst[:, t, :], src(t), meanvar[:, t, 0:1], rstd[:, t:t + 1],
                                    ALU.subtract, ALU.mult).then_inc(norm_ready[k], 1)

            def phi_keys(g, n):
                v.wait_ge(k_exp, g * PAIRS + n + 1)
                v.scalar_tensor_tensor(kT[:, n, :], Z[n % 4][:, :], 0.0, ex[:, n % 2, :], ALU.max, ALU.add).then_inc(k_phi, 1)

            def phi_queries(g, n):
                v.wait_ge(q_exp, g * PAIRS + n + 1)
                v.scalar_tensor_tensor(qT[0:DH, n, 0, :], Z[n % 4][0:DH, :], 0.0, ex[0:DH, n % 2, :],
                                       ALU.max, ALU.add).then_inc(q_phi, 1)
                v.scalar_tensor_tensor(qT[DH:P, n, 1, :], Z[n % 4][DH:P, :], 0.0, ex[DH:P, n % 2, :],
                                       ALU.max, ALU.add).then_inc(q_phi, 1)

            def mask(g, ch, q):
                v.wait_ge(kq_full, g * 16 + 4 * ch + q + 1)
                v.tensor_tensor(att[:, 4 * q:4 * q + 4, :], KQ[q % 2][:, :].rearrange("p (h s) -> p h s", h=4),
                                causal[:, :, :], ALU.mult).then_inc(masked, 1)

            def update(g, ch, half, use):
                v.wait_ge(u_full, g * U_USES + use + 1)
                rows = slice(4 * half, 4 * half + 4)
                v.tensor_tensor(state[:, (ch + 1) % 2, rows, :], U[:, :].rearrange("p (h w) -> p h w", h=4),
                                state[:, ch % 2, rows, :], ALU.add).then_inc(u_taken, 1)

            def divide(g, base, ch, half):
                n = 2 * ch + half
                if n or not isinstance(g, int) or g:
                    v.wait_ge(o_ready, g * 8 + n)
                v.wait_ge(nd_full, g * 8 + n + 1)
                v.tensor_scalar(den[:, :], DEN[:, :], EPS_DEN, None, ALU.max).then_inc(den_taken, 1)
                v.wait_ge(den_taken, g * 8 + n + 1)
                own.mark(v.reciprocal(den[:, :], den[:, :]))
                v.wait_ge(dve, own.value(base))
                v.wait_ge(num_taken, g * 8 + n + 1)
                rows = slice(4 * half, 4 * half + 4)
                v.tensor_tensor(oT[:, rows, :], oT[:, rows, :], den[:, :].rearrange("p (h s) -> p h s", h=4),
                                ALU.mult).then_inc(o_ready, 1)

            def residual(g, ch, use):
                v.wait_ge(u_full, g * U_USES + use + 1)
                if ch == 0:
                    v.wait_ge(x_ld, g * 16 + 16)
                v.tensor_tensor(x1[:, ch, :], U[:, 0:D], x[:, ch, :], ALU.add).then_inc(u_taken, 1)

            def next_values(g):
                v.wait_ge(v2_full, g + 1)
                v.wait_ge(parts_free, 1 + g)
                for t in range(NT):
                    v.tensor_tensor(vst[:, t, :, 0:KPH], V2[:, t * LAT:(t + 1) * LAT].rearrange("p (h d) -> p h d", h=H),
                                    vb[:, :].rearrange("p (h d) -> p h d", h=H), ALU.add).then_inc(v2_taken, 1)

            def split(g, base):
                for i in range(2):
                    v.wait_ge(qk_taken, g * 2 + i + 1)
                    own.mark(v.tensor_copy(parts[:, i, 0, :], qk[:, i, :]))
                    v.wait_ge(dve, own.value(base))
                    own.mark(v.tensor_tensor(rest[:, :], qk[:, i, :], parts[:, i, 0, :], ALU.subtract))
                    v.wait_ge(dve, own.value(base))
                    own.mark(v.tensor_copy(parts[:, i, 1, :], rest[:, :]))
                    v.wait_ge(dve, own.value(base))
                    v.tensor_tensor(parts[:, i, 2, :], rest[:, :], parts[:, i, 1, :], ALU.subtract).then_inc(parts_ready, 1)

            def x_tile(t):
                return x_norm[:, t, :]

            def y_tile(t):
                return y[:, t, :]

            def body(g, first, last):
                own.n = 10
                for n in range(PAIRS):
                    phi_queries(g, n)
                if first:
                    v.wait_ge(made, 5)
                for ch in range(NT):
                    mask(g, ch, 0)
                    mask(g, ch, 1)
                    update(g, ch, 0, 3 * ch - (ch > 0))
                    mask(g, ch, 2)
                    mask(g, ch, 3)
                    if ch == 0 and not first:
                        statistics(2, g - 1, g, y_tile)
                    if ch == 1 and not last:
                        v.wait_ge(x_norm_ld, g * 16 + 16)
                        statistics(0, g + 1, g, x_tile)
                    if ch:
                        residual(g, ch - 1, 3 * ch)
                    divide(g, g, ch, 0)
                    update(g, ch, 1, 3 * ch + 1)
                    if ch == 0 and not first:
                        v.wait_ge(x3_free, g)
                        normalise(2, g - 1, y_tile, x3)
                        v.wait_ge(norm_ready[2], g * NT)
                    if ch == 1 and not last:
                        normalise(0, g + 1, x_tile, xn)
                    if ch == NT - 1 and not last:
                        split_feat(g + 1, 0, g)
                    divide(g, g, ch, 1)
                if not last:
                    split_feat(g + 1, 1, g)
                if not first:
                    next_values(g - 1)
                residual(g, NT - 1, 3 * NT - 1)
                v.wait_ge(u_taken, g * U_USES + U_USES)
                statistics(1, g, g, y_tile)
                if not last:
                    phi_keys(g + 1, 0)
                normalise(1, g, y_tile, xn)
                if not last:
                    for n in range(1, PAIRS):
                        phi_keys(g + 1, n)
                    own.mark(v.tensor_scalar(state[:, 0, :, :], state[:, 0, :, :], keep[:, bass.ds(g, 1)], None, ALU.mult))
                if not first:
                    split(g - 1, g)
                for t in range(NT):
                    v.wait_ge(ffn_full, g * NT + t + 1)
                    own.mark(v.tensor_tensor(y[:, t, :], [NUM, DEN][t % 2][:, 0:D], x1[:, t, :], ALU.add))
                    v.wait_ge(dve, own.value(g))
                    v.tensor_tensor(y[:, t, :], y[:, t, :], x[:, t, :], ALU.add).then_inc(ffn_taken, 1)
                v.wait_ge(ffn_taken, g * NT + NT)
                if first:
                    v.sem_inc(dve, 10 + own.per - own.n)
                else:
                    assert last or own.n == 10 + own.per, own.n

            for tile, value in ((vt, 1.0), (state, 0.0), (vst, 1.0)):
                v.memset(tile[:, :, :, :], value).then_inc(set_up, 1)
            v.wait_ge(x_first_ld, 16)
            statistics(0, 0, 0, x_tile)
            normalise(0, 0, x_tile, xn)
            split_input(0)
            for c in range(DC):
                split_feat(0, c, 0)
            split_input(1)
            for n in range(PAIRS):
                phi_keys(0, n)
            v.wait_ge(set_up, 7)
            v.wait_ge(qT_clear, 1)
            v.wait_ge(small_ld, SMALL)
            body(0, True, False)
            with v.Fori(1, STEPS - 1) as g:
                body(g, False, False)
            body(STEPS - 1, False, True)
            statistics(2, STEPS - 1, STEPS - 1, y_tile)
            v.wait_ge(x3_free, STEPS)
            normalise(2, STEPS - 1, y_tile, x3)
            next_values(STEPS - 1)
            split(STEPS - 1, STEPS - 1)

        @block.scalar
        def _(s):
            s.wait_ge(small_ld, SMALL)

            def take_turned(k, g, c, dst, gain=None, shift=None):
                s.wait_ge(norm_turned[k], g * DC + c + 1)
                if gain is None:
                    s.activation(dst[:, c, :], TURNED[k][c][:, :], ACT.Copy).then_inc(norm_taken[k], 1)
                else:
                    s.activation(dst[:, c, :], TURNED[k][c][:, :], ACT.Identity, bias=shift[:, c:c + 1], scale=gain[:, c:c + 1])\
                     .then_inc(norm_taken[k], 1)

            def exponential(full, done, g, n, use):
                s.wait_ge(full, g * PAIRS + n + 1)
                s.activation(ex[:, n % 2, :], Z[n % 4][:, :], ACT.Relu, scale=-1.0).then_inc(below_ready, 1)
                s.wait_ge(below_ready, use + 1)
                s.activation(ex[:, n % 2, :], ex[:, n % 2, :], ACT.Exp, scale=-1.0).then_inc(done, 1)

            def keys(g, ns):
                for n in ns:
                    if n >= 2:
                        s.wait_ge(k_phi, g * PAIRS + n - 1)
                    exponential(k_full, k_exp, g, n, g * 2 * PAIRS + n)

            def next_queries_keys(g):
                for i, bias in enumerate((qb, kb)):
                    s.wait_ge(qk_full, g * 2 + i + 1)
                    s.activation(qk[:, i, :], A[i][:, :], ACT.Identity, bias=bias[:, :]).then_inc(qk_taken, 1)

            def body(g, first, last):
                for n in range(PAIRS):
                    if n >= 2:
                        s.wait_ge(q_phi, g * 2 * PAIRS + 2 * (n - 1))
                    elif n == 0:
                        s.wait_ge(k_phi, g * PAIRS + PAIRS)
                    exponential(q_full, q_exp, g, n, g * 2 * PAIRS + PAIRS + n)
                for ch in range(NT):
                    for half in range(2):
                        s.wait_ge(v_full, g * 8 + 2 * ch + half + 1)
                        s.activation(vt[:, 8 * half:8 * half + 8, 0, :], A[half][:, :].rearrange("p (h d) -> p h d", h=8),
                                     ACT.Copy).then_inc(v_taken, 1)
                        s.wait_ge(keys_turned, g * 8 + 2 * ch + half + 1)
                        s.activation(kt[:, 8 * half:8 * half + 8, :].rearrange("p h d -> p (h d)"), TR[:, :],
                                     ACT.Copy).then_inc(keys_taken, 1)
                    for half in range(2):
                        if ch == NT - 2 and not first:
                            take_turned(2, g - 1, half, feat2)
                        if ch == NT - 1 and not last:
                            take_turned(0, g + 1, half, feat, ln1g, ln1b)
                        s.wait_ge(nd_full, g * 8 + 2 * ch + half + 1)
                        s.activation(oT[:, 4 * half:4 * half + 4, :], NUM[:, :].rearrange("p (h s) -> p h s", h=4),
                                     ACT.Copy).then_inc(num_taken, 1)
                if not first:
                    next_queries_keys(g - 1)
                if not last:
                    s.wait_ge(q_phi, (g + 1) * 2 * PAIRS)
                    keys(g + 1, range(K_EARLY))
                for c in range(DC):
                    take_turned(1, g, c, feat2, ln2g, ln2b)
                if not last:
                    keys(g + 1, range(K_EARLY, PAIRS))
                for j in range(FC):
                    s.wait_ge(hidden_full, g * FC + j + 1)
                    s.activation(fT[:, j, :], A[j % 2][:, :], ACT.Gelu).then_inc(hidden_ready, 1)

            for c in range(DC):
                take_turned(0, 0, c, feat, ln1g, ln1b)
            keys(0, range(PAIRS))
            s.wait_ge(set_up, 7)
            body(0, True, False)
            with s.Fori(1, STEPS - 1) as g:
                body(g, False, False)
            body(STEPS - 1, False, True)
            for c in range(DC):
                take_turned(2, STEPS - 1, c, feat2)
            next_queries_keys(STEPS - 1)

        @block.tensor
        def _(pe):
            def turn(blocks, full, into=TR):
                for i, block_in in enumerate(blocks):
                    last = pe.transpose(into[:, i * P:(i + 1) * P], block_in, ident[:, :])
                last.then_inc(full, 1)

            def turn_norm(k, g, c, src):
                pe.wait_ge(norm_ready[k], g * NT + NT)
                if c and TURNED[k][c] is TURNED[k][c - 1]:
                    pe.wait_ge(norm_taken[k], g * DC + c)
                turn([src[:, t, c * P:(c + 1) * P] for t in range(NT)], norm_turned[k], TURNED[k][c])

            def project(dst, lhs, rhs, full, chunks=DC):
                for c in range(chunks):
                    last = pe.matmul(dst, lhs(c), rhs(c), start=(c == 0), stop=(c == chunks - 1))
                last.then_inc(full, 1)

            def split_project(dst, lhs, rhs, full):
                products = [(c, i, j) for c in range(DC) for i, j in ((0, 0), (0, 1), (1, 0))]
                for k, (c, i, j) in enumerate(products):
                    last = pe.matmul(dst, lhs(i, c), rhs(j, c), start=(k == 0), stop=(k == len(products) - 1))
                last.then_inc(full, 1)

            def pair_projection(w, n, full):
                split_project(Z[n % 4][:, :], lambda i, c: w[:, i, c, n * P:(n + 1) * P],
                              lambda j, c: feat_parts[:, j, c, :], full)

            def key_projection(g, n):
                if n == 0:
                    pe.wait_ge(feat_split, g * DC + DC)
                if n == 3 and (not isinstance(g, int) or g >= 2):
                    pe.wait_ge(v2_taken, (g - 1) * NT)
                if n >= 4:
                    pe.wait_ge(k_phi, g * PAIRS + n - 3)
                pair_projection(wk, n, k_full)

            def query_projection(g, n):
                if n == 0:
                    pe.wait_ge(k_phi, g * PAIRS + PAIRS)
                if n >= 4:
                    pe.wait_ge(q_phi, g * 2 * PAIRS + 2 * (n - 3))
                pair_projection(wq, n, q_full)

            def values(g, ch, half):
                if ch == 0:
                    pe.wait_ge(q_phi, g * 2 * PAIRS + 2 * (PAIRS - 3 + half))
                else:
                    pe.wait_ge(v_taken, g * 8 + 2 * ch + half - 1)
                project(A[half][:, :], lambda c: feat[:, c, ch * P:(ch + 1) * P],
                        lambda c: wv[:, c, half * 512:half * 512 + 512], v_full)

            def turn_keys(g, ch, half):
                if ch or half:
                    pe.wait_ge(keys_taken, g * 8 + 2 * ch + half)
                turn([kT[:, 4 * half + i, ch * P:(ch + 1) * P] for i in range(4)], keys_turned)

            def scores(g, ch, q):
                if ch or q >= 2:
                    pe.wait_ge(masked, g * 16 + 4 * ch + q - 1)
                else:
                    pe.wait_ge(q_phi, g * 2 * PAIRS + 2 * (PAIRS - 1 + q))
                for i in range(2):
                    pair = 2 * q + i
                    last = pe.matmul(KQ[q % 2][:, i * 2 * P:(i + 1) * 2 * P].rearrange("p (h s) -> p h s", h=2),
                                     kT[:, pair, ch * P:(ch + 1) * P], qT[:, pair, :, ch * P:(ch + 1) * P],
                                     start=True, stop=True)
                last.then_inc(kq_full, 1)

            def free_update_bank(g, use):
                if use or not isinstance(g, int) or g:
                    pe.wait_ge(u_taken, g * U_USES + use)

            def state_update(g, ch, half, use):
                free_update_bank(g, use)
                pe.wait_ge(keys_taken, g * 8 + 2 * ch + half + 1)
                pe.wait_ge(v_taken, g * 8 + 2 * ch + half + 1)
                for i in range(4):
                    for o in range(2):
                        h = 8 * half + 2 * i + o
                        last = pe.matmul(U[o * DH:(o + 1) * DH, i * P:(i + 1) * P], kt[:, h, :],
                                         vt[:, h, :, :].rearrange("p a d -> p (a d)"), start=True, stop=True)
                last.then_inc(u_full, 1)

            def outputs(g, ch, half):
                n = 2 * ch + half
                if n:
                    pe.wait_ge(num_taken, g * 8 + n)
                    pe.wait_ge(den_taken, g * 8 + n)
                    pe.wait_ge(u_taken, g * U_USES + (3 * ch - 1 if half == 0 else 3 * ch + 1))
                elif not isinstance(g, int) or g:
                    pe.wait_ge(ffn_taken, g * NT)
                pe.wait_ge(masked, g * 16 + 4 * ch + 2 * half + 2)
                s0 = ch % 2
                for i in range(4):
                    pair = 4 * half + i
                    cols = slice(i * P, (i + 1) * P)
                    for dst, lhs, w in ((NUM, lambda h: vt[:, h, 0, :], slice(0, DH)),
                                        (DEN, lambda h: ones[:, :], slice(DH, 2 * DH))):
                        for o in range(2):
                            pe.matmul(dst[o * DH:(o + 1) * DH, cols], lhs(2 * pair + o), att[:, 2 * pair + o, :],
                                      start=True, stop=False)
                        for o in range(2):
                            last = pe.matmul(dst[o * DH:(o + 1) * DH, cols], state[:, s0, pair, w],
                                             qT[:, pair, o, ch * P:(ch + 1) * P], start=False, stop=True)
                last.then_inc(nd_full, 1)

            def attention_out(g, ch, use):
                free_update_bank(g, use)
                pe.wait_ge(o_ready, g * 8 + 2 * ch + 2)
                project(U[:, 0:D], lambda c: oT[:, c, :], lambda c: wo[:, c, :], u_full, PAIRS)

            def next_attention(g, taken):
                pe.wait_ge(norm_taken[2], g * DC + DC)
                for t in range(NT):
                    for c in range(DC):
                        last = pe.matmul(V2[:, t * LAT:(t + 1) * LAT], feat2[:, c, t * P:(t + 1) * P], vw[:, c, :],
                                         start=(c == 0), stop=(c == DC - 1))
                last.then_inc(v2_full, 1)
                pe.wait_ge(v_taken, taken)
                for i, w in enumerate((qw, kw)):
                    project(A[i][:, :], lambda c: w[:, c, :], lambda c: feat2[:, c, :], qk_full)

            def body(g, first, last):
                for n in range(PAIRS):
                    query_projection(g, n)
                for ch in range(NT):
                    values(g, ch, 0)
                    if ch == NT - 1 and not first:
                        pe.wait_ge(norm_taken[2], g * DC)
                    turn_keys(g, ch, 0)
                    values(g, ch, 1)
                    scores(g, ch, 0)
                    turn_keys(g, ch, 1)
                    scores(g, ch, 1)
                    state_update(g, ch, 0, 3 * ch - (ch > 0))
                    scores(g, ch, 2)
                    scores(g, ch, 3)

                    def turn_another(c):
                        if c == 0:
                            pe.wait_ge(keys_taken, g * 8 + 2 * ch + 2)
                        if ch == NT - 2 and not first:
                            turn_norm(2, g - 1, c, x3)
                        if ch == NT - 1 and not last:
                            turn_norm(0, g + 1, c, xn)

                    turn_another(0)
                    if ch:
                        attention_out(g, ch - 1, 3 * ch)
                    outputs(g, ch, 0)
                    state_update(g, ch, 1, 3 * ch + 1)
                    turn_another(1)
                    outputs(g, ch, 1)
                if not first:
                    next_attention(g - 1, g * 8 + 8)
                attention_out(g, NT - 1, 3 * NT - 1)

                if not last:
                    pe.wait_ge(v_taken, g * 8 + 8)
                    if not first:
                        pe.wait_ge(qk_taken, g * 2)
                    for n in range(K_EARLY):
                        key_projection(g + 1, n)
                for c in range(DC):
                    turn_norm(1, g, c, xn)
                if not last:
                    for n in range(K_EARLY, PAIRS):
                        key_projection(g + 1, n)
                pe.wait_ge(norm_taken[1], g * DC + DC)
                for j in range(FC):
                    if j < 2:
                        if last:
                            pe.wait_ge(qk_taken, g * 2)
                        else:
                            pe.wait_ge(k_phi, (g + 1) * PAIRS + PAIRS - 3 + j)
                    else:
                        pe.wait_ge(hidden_ready, g * FC + j - 1)
                    project(A[j % 2][:, :], lambda c: wf1[:, c, j * P:(j + 1) * P], lambda c: feat2[:, c, :], hidden_full)
                for t in range(NT):
                    if t == 0:
                        pe.wait_ge(num_taken, g * 8 + 8)
                        pe.wait_ge(den_taken, g * 8 + 8)
                    elif t >= 2:
                        pe.wait_ge(ffn_taken, g * NT + t - 1)
                    for j in range(FC):
                        if t == 0:
                            pe.wait_ge(hidden_ready, g * FC + j + 1)
                        last_mm = pe.matmul([NUM, DEN][t % 2][:, 0:D], fT[:, j, t * P:(t + 1) * P], wf2[:, j, :],
                                            start=(j == 0), stop=(j == FC - 1))
                    last_mm.then_inc(ffn_full, 1)

            pe.wait_ge(made, 3)
            for c in range(DC):
                turn_norm(0, 0, c, xn)
            pe.wait_ge(in_split[0], 8)
            for n in range(PAIRS):
                key_projection(0, n)
            pe.wait_ge(w_ld, W_ALL)
            pe.wait_ge(in_split[1], 8)
            pe.wait_ge(set_up, 7)
            body(0, True, False)
            with pe.Fori(1, STEPS - 1) as g:
                body(g, False, False)
            body(STEPS - 1, False, True)
            for c in range(DC):
                turn_norm(2, STEPS - 1, c, x3)
            next_attention(STEPS - 1, STEPS * 8)


GROUP = 4
GROUPS = B * H // GROUP
HEADS = B * H
TC = T // P
SB = T // 512
STACK = PARTS * PARTS * KPH
ROWS = 96
LEAD = TC + 4
VM = 32
STACK_DMAS = 2 * PARTS + 1


def softmax_attention_stage(nc, a, scratch, w1, w2):
    ctx = ExitStack()
    with ctx:
        def sb(name, shape, dt=F32):
            return ctx.enter_context(nc.sbuf_tensor(name, shape, dt))

        def ps(name, shape, dt=F32):
            return ctx.enter_context(nc.psum_tensor(name, shape, dt))

        def sem(name):
            return ctx.enter_context(nc.semaphore(name))

        qs = [sb(f"qs{i}", [P, T], BF16) for i in range(GROUP)]
        ks = [sb(f"ks{i}", [P, T], BF16) for i in range(GROUP)]
        zeros, minus_ones = sb("zeros", [PARTS, T], BF16), sb("minus_ones", [PARTS, T], BF16)
        identb = sb("identb", [P, P], BF16)
        vh = sb("vh", [P, 2, TC, VM])
        w_in = sb("w_in", [P, 4, 512])
        pt = sb("pt", [P, 2, T])
        tops = sb("tops", [P, TC, 2])
        top = sb("top", [P, TC])
        top_parts = sb("top_parts", [P, PARTS, TC], BF16)
        top_rows = sb("top_rows", [PARTS * TC, P], BF16)
        av_out = sb("av_out", [P, 2, 512])

        S1 = [ps(f"raw{i}", [P, 1024]) for i in range(2)]
        S2 = [ps(f"shifted{i}", [P, 512]) for i in range(2)]
        AV = ps("av", [P, 512])
        TR = ps("turned_tops", [PARTS * TC, P], BF16)

        stack_ld = [sem(f"stack_ld{i}") for i in range(GROUP)]
        shift_ld = [sem(f"shift_ld{i}") for i in range(GROUP)]
        v_ld, av_stored = [sem(f"v_ld{i}") for i in range(2)], sem("av_stored")
        w_ld, w_split = sem("b_w_ld"), sem("w_split")
        passed_sp, passed_pe = sem("b_passed_sp"), sem("b_passed_pe")
        b_made, padded = sem("b_made"), sem("padded")
        vh_clear = sem("vh_clear")
        minus_ld = [sem(f"minus_ld{i}") for i in range(GROUP)]
        raw_full, raw_taken = sem("raw_full"), sem("raw_taken")
        tops_ready, tops_turned, rows_ready = sem("tops_ready"), sem("tops_turned"), sem("rows_ready")
        shifted_full, exp_done = sem("shifted_full"), sem("exp_done")
        av_tile = sem("av_tile")
        av_taken = sem("av_taken")
        av_free = sem("av_free")
        dve = sem("b_dve")
        block = ctx.enter_context(nc.Block())

        @block.sync
        def _(sp):

            def load_values(n, u):
                wait_apart(sp, av_free, n + 1, passed_sp)
                sp.dma_start(vh[:, u, :, 0:VW], scratch["v"][:, :, bass.ds(n * VW, VW)],
                             allow_slow_non_contiguous=True).then_inc(v_ld[u], 16)

            def load_weights(e):
                sp.dma_start(w_in[:, 0:2, :], a["L0_ffn_w1"][bass.ds(e, 1)].rearrange("e (c p) n -> p (e c) n", p=P)).then_inc(w_ld, 16)
                sp.dma_start(w_in[:, 2:4, :].rearrange("p i (j d) -> p (i j) d", d=D),
                             a["L0_ffn_w2"][bass.ds(e, 1)].rearrange("e (j p) d -> p (e j) d", p=P)).then_inc(w_ld, 16)

            def load_stacks(n, u):
                for i in range(PARTS):
                    r = i * PARTS * KPH
                    q_rows = scratch["qk"][0].rearrange("i b p s -> i (b p) s")[:, bass.ds(n * KPH, KPH), :]
                    k_rows = scratch["qk"][1, i:i + 1].rearrange("i b p s -> i (b p) s")[:, bass.ds(n * KPH, KPH), :]
                    sp.dma_start(qs[u][r:r + PARTS * KPH, :], q_rows).then_inc(stack_ld[u], 16)
                    sp.dma_start(ks[u][r:r + PARTS * KPH, :], k_rows.broadcast_to([PARTS, KPH, T])).then_inc(stack_ld[u], 16)
                sp.dma_start(qs[u][STACK:STACK + PARTS, :], zeros[:, :]).then_inc(stack_ld[u], 16)

            def load_shift(n, u):
                wait_apart(sp, rows_ready, n + 1, passed_sp)
                sp.dma_start(qs[u][STACK:STACK + PARTS, :].rearrange("r (c s) -> r c s", c=TC), top_rows[:, :])\
                  .then_inc(shift_ld[u], 16)

            for u in range(GROUP):
                sp.wait_ge(padded, 1 + 2 * (u + 1))
                sp.wait_ge(b_made, 3)
                load_stacks(u, u)
                sp.dma_start(ks[u][STACK:STACK + PARTS, :], minus_ones[:, :]).then_inc(minus_ld[u], 16)
            sp.wait_ge(vh_clear, 1)
            for u in range(2):
                load_values(u, u)
            load_weights(0)
            load_shift(0, 0)
            with sp.Fori(0, GROUPS - 1) as g:
                for u in range(GROUP):
                    n = g * GROUP + u
                    load_shift(n + 1, (u + 1) % GROUP)
                    wait_apart(sp, shifted_full, (n + 1) * (TC * SB), passed_sp)
                    load_stacks(n + GROUP, u)
                    load_values(n + 2, u % 2)
                    if u == GROUP - 2:
                        wait_apart(sp, w_split, (g + 1) * 8, passed_sp)
                        load_weights(g + 1)
            for u in range(GROUP - 1):
                n = HEADS - GROUP + u
                load_shift(n + 1, u + 1)
                if u < 2:
                    load_values(n + 2, u)

        @block.gpsimd
        def _(pool):
            pool.sem_inc(av_free, 2)
            pool.memset(minus_ones[:, :], -1.0).then_inc(b_made, 1)
            pool.wait_ge(b_made, 1)
            pool.memset(identb[:, :], 0.0).then_inc(b_made, 1)
            pool.wait_ge(b_made, 2)
            pool.affine_select(out=identb[:, :], in_=identb[:, :], compare_op=ALU.not_equal, fill=1.0, base=0,
                               pattern=[[-1, P]], channel_multiplier=1).then_inc(b_made, 1)
            def store(n, u):
                pool.wait_ge(av_taken, n + 1)
                for q in range(SB):
                    pool.dma_start(scratch["av"][bass.ds(n, 1), q].rearrange("o w s -> (o w) s"),
                                   av_out[q * VM:q * VM + VW, u, :]).then_inc(av_stored, 16)
                pool.wait_ge(av_stored, n * (16 * SB) + 16 * SB)
                pool.sem_inc(av_free, 1)

            with pool.Fori(0, HEADS // 2) as i:
                for u in range(2):
                    store(i * 2 + u, u)
            pool.wait_ge(av_stored, 16 * SB * HEADS)

        @block.vector
        def _(v):
            v.memset(zeros[:, :], 0.0).then_inc(padded, 1)
            for u in range(GROUP):
                for stack in (qs[u], ks[u]):
                    v.memset(stack[64:ROWS, :], 0.0).then_inc(padded, 1)
            v.memset(vh[:, :, :, :], 0.0).then_inc(vh_clear, 1)

            def tile_maxima(n, c):
                for half in range(2):
                    v.wait_ge(raw_full, n * (2 * TC) + 2 * c + half + 1)
                    v.tensor_reduce(tops[:, c, half:half + 1], S1[half][:, :], axis=AX.X, op=ALU.max).then_inc(raw_taken, 1)

            def split_tops(n):
                v.wait_ge(raw_taken, (n + 1) * (2 * TC))
                v.tensor_tensor(top[:, :], tops[:, :, 0], tops[:, :, 1], ALU.max).then_inc(dve, 1)
                v.wait_ge(dve, n * 4 + 1)
                v.tensor_copy(top_parts[:, 0, :], top[:, :]).then_inc(dve, 1)
                for i in range(1, PARTS):
                    v.wait_ge(dve, n * 4 + 2 * i)
                    if i < PARTS - 1:
                        v.tensor_tensor(top[:, :], top[:, :], top_parts[:, i - 1, :], ALU.subtract).then_inc(dve, 1)
                        v.wait_ge(dve, n * 4 + 2 * i + 1)
                        v.tensor_copy(top_parts[:, i, :], top[:, :]).then_inc(dve, 1)
                    else:
                        v.tensor_tensor(top_parts[:, i, :], top[:, :], top_parts[:, i - 1, :], ALU.subtract).then_inc(tops_ready, 1)

            def take_rows(n):
                v.wait_ge(tops_turned, n + 1)
                v.tensor_copy(top_rows[:, :], TR[:, :]).then_inc(rows_ready, 1)

            def split_weights(g, u, low):
                w = w1[:, bass.ds(g, 1), u, :, :] if u < 2 else w2[:, bass.ds(g, 1), u - 2, :, :]
                high_part, low_part = (w[:, :, k, :].rearrange("p e n -> p (e n)") for k in range(2))
                if not low:
                    v.wait_ge(w_ld, g * 32 + 32)
                    v.tensor_copy(high_part, w_in[:, u, :]).then_inc(w_split, 1)
                else:
                    v.wait_ge(w_split, g * 8 + 2 * u + 1)
                    v.tensor_tensor(low_part, w_in[:, u, :], high_part, ALU.subtract).then_inc(w_split, 1)

            def head(g, u, last=False):
                n = g * GROUP + u
                for c in range(2, TC):
                    tile_maxima(n, c)
                    if c in (10, 13):
                        split_weights(g, u, c == 13)
                split_tops(n)
                if not last:
                    for c in range(2):
                        tile_maxima(n + 1, c)
                take_rows(n)

            for c in range(2):
                tile_maxima(0, c)
            with v.Fori(0, GROUPS - 1) as g:
                for u in range(GROUP):
                    head(g, u)
            for u in range(GROUP):
                head(GROUPS - 1, u, u == GROUP - 1)

        @block.scalar
        def _(s):
            def exponentials(g, r):
                u, c = divmod(r, TC)
                n = g * GROUP + u
                for q in range(SB):
                    if q == 0 and not (isinstance(g, int) and g == 0 and r < 2):
                        s.wait_ge(av_tile, 1 + n * TC + c - 1)
                    s.wait_ge(shifted_full, n * (TC * SB) + SB * c + q + 1)
                    s.activation(pt[:, c % 2, q * 512:(q + 1) * 512], S2[q % 2][:, :], ACT.Exp, scale=KPH ** -0.5)\
                     .then_inc(exp_done, 1)
                    if q == SB - 1 and c == 0 and r:
                        take_output(g, u - 1)

            def take_output(g, u):
                n = g * GROUP + u
                s.wait_ge(av_tile, 1 + (n + 1) * TC)
                s.wait_ge(av_free, n + 1)
                s.activation(av_out[:, u % 2, :], AV[:, :], ACT.Copy).then_inc(av_taken, 1)

            exponentials(0, 0)
            with s.Fori(0, GROUPS - 1) as g:
                for r in range(1, GROUP * TC + 1):
                    exponentials(g, r)
            for r in range(1, GROUP * TC):
                exponentials(GROUPS - 1, r)
            take_output(GROUPS - 1, GROUP - 1)

        @block.tensor
        def _(pe):
            from_one(pe, av_tile)
            pe.wait_ge(b_made, 3)

            def raw(g, r, k):
                u, c = divmod(r, TC)
                n = g * GROUP + u
                if isinstance(g, int) and n >= HEADS:
                    if n == HEADS and c == 1 and k == 0:
                        turn_tops(g, u - 1)
                    return
                if c == 1 and k == 0 and r > 1:
                    turn_tops(g, u - 1)
                if c == 0 and k == 0:
                    m = n // GROUP if isinstance(n, int) else g + u // GROUP
                    pe.wait_ge(minus_ld[u % GROUP], 16)
                    pe.wait_ge(stack_ld[u % GROUP], (m + 1) * (16 * STACK_DMAS))
                half, part = divmod(k, 2)
                if part == 0:
                    unit = 2 * c + half
                    if not (isinstance(n, int) and n == 0 and unit < 2):
                        pe.wait_ge(raw_taken, n * (2 * TC) + unit - 1)
                last = pe.matmul(S1[half][:, part * 512:(part + 1) * 512], qs[u % GROUP][0:ROWS, c * P:(c + 1) * P],
                                 ks[u % GROUP][0:ROWS, k * 512:(k + 1) * 512], start=True, stop=True)
                if part:
                    last.then_inc(raw_full, 1)

            def turn_tops(g, u):
                wait_apart(pe, tops_ready, g * GROUP + u + 1, passed_pe)
                pe.transpose(TR[:, :], top_parts[:, :, :].rearrange("p i c -> p (i c)"), identb[:, :]).then_inc(tops_turned, 1)

            def shifted(g, r, q):
                u, c = divmod(r, TC)
                n = g * GROUP + u
                if c == 0 and q == 0:
                    m = n // GROUP if isinstance(n, int) else g + u // GROUP
                    pe.wait_ge(shift_ld[u % GROUP], m * 16 + 16)
                if not (isinstance(n, int) and n == 0 and c == 0 and q < 2):
                    pe.wait_ge(exp_done, n * (TC * SB) + SB * c + q - 1)
                pe.matmul(S2[q % 2][:, :], ks[u % GROUP][0:ROWS, c * P:(c + 1) * P],
                          qs[u % GROUP][0:ROWS, q * 512:(q + 1) * 512], start=True, stop=True).then_inc(shifted_full, 1)

            def weigh(g, r):
                u, c = divmod(r, TC)
                n = g * GROUP + u
                if c == 0:
                    m = n // 2 if isinstance(n, int) else g * (GROUP // 2) + u // 2
                    pe.wait_ge(v_ld[u % 2], m * 16 + 16)
                    if r:
                        pe.wait_ge(av_taken, n)
                pe.wait_ge(exp_done, n * (TC * SB) + SB * (c + 1))
                for q in range(SB):
                    last = pe.matmul(AV[q * VM:(q + 1) * VM, :], vh[:, u % 2, c, :], pt[:, c % 2, q * 512:(q + 1) * 512],
                                     start=(c == 0), stop=(c == TC - 1))
                last.then_inc(av_tile, 1)

            def tile_step(g, r):
                for half in range(2):
                    for q in range(2):
                        shifted(g, r, 2 * half + q)
                    if half == 0:
                        for k in range(SB):
                            raw(g, r + LEAD, k)
                    elif r:
                        weigh(g, r - 1)

            for r in range(LEAD):
                for k in range(SB):
                    raw(0, r, k)
            tile_step(0, 0)
            with pe.Fori(0, GROUPS - 1) as g:
                for r in range(1, GROUP * TC + 1):
                    tile_step(g, r)
            for r in range(1, GROUP * TC):
                tile_step(GROUPS - 1, r)
            weigh(GROUPS - 1, GROUP * TC - 1)


def experts_stage(nc, a, scratch, w1, w2, out):
    ctx = ExitStack()
    with ctx:
        def sb(name, shape, dt=F32):
            return ctx.enter_context(nc.sbuf_tensor(name, shape, dt))

        def bank(name):
            return ctx.enter_context(nc.psum_tensor(name, [P, 512], F32))

        def sem(name):
            return ctx.enter_context(nc.semaphore(name))

        ow, rw = sb("ow", [P, D]), sb("rw", [P, DC, E])
        ob, b1 = sb("ob", [P, DC]), sb("b1", [P, E, EC])
        rb, b2 = sb("rb", [P, NT, E]), sb("b2", [E, D])
        ident = sb("c_ident", [P, P])
        iota_i, iota = sb("iota_i", [P, E], mybir.dt.int32), sb("iota", [P, E])
        minus_half = sb("c_minus_half", [P, NT])
        x3 = sb("c_x3", [P, NT, D])
        num, den = sb("c_num", [LAT, ST]), sb("c_den", [LAT, ST])
        aoT = sb("aoT", [LAT, ST])
        mlaT = sb("mlaT", [P, DC, ST])
        mla_parts = sb("mla_parts", [P, 2, DC, ST], F32R)
        logits = sb("logits", [P, NT, E])
        probs = sb("probs", [P, NT, E])
        small = sb("small", [P, NT])
        weight_sum = sb("weight_sum", [P, NT])
        best = sb("best", [P, NT, 8])
        best_at = sb("best_at", [P, NT, 8], U32)
        at_f = sb("at_f", [P, NT, 2])
        weight = sb("weight", [P, NT, 2])
        chosen = sb("chosen", [P, 2, NT, E])
        comb = sb("comb", [P, NT, E])
        combT = sb("combT", [E, ST])
        gelu = sb("gelu", [P, 2, ST])
        h1 = sb("h1", [P, 2, 2, EC, ST], F32R)
        moe = sb("moe", [P, NT, D])
        stats = sb("c_stats", [P, NT, 6])
        meanvar = sb("c_meanvar", [P, NT, 2])
        var_eps, rstd = sb("c_var_eps", [P, NT]), sb("c_rstd", [P, NT])
        res = sb("res", [P, NT, D])

        A = [bank("h1_0"), bank("h1_1")]
        H2 = [bank(f"h2_{t}") for t in range(NT)]
        R, CT = bank("router"), bank("comb_ps")

        c_ld, c_small, ao_ld, x3_ld, out_stored = (sem(n) for n in ("c_ld", "c_small", "ao_ld", "x3_ld", "out_stored"))
        c_made = sem("c_made")
        res_free = sem("res_free")
        passed_sp, passed_v = sem("c_passed_sp"), sem("c_passed_v")
        ao_ready = sem("ao_ready")
        acc_full, acc_taken = sem("c_acc_full"), sem("c_acc_taken")
        mla_split = sem("mla_split")
        h1_split = sem("h1_split")
        h2_full, h2_taken = sem("h2_full"), sem("h2_taken")
        logits_full, logits_ready, exp_ready, comb_ready = (sem(n) for n in ("logits_full", "logits_ready", "c_exp", "comb_ready"))
        combT_full, combT_ready = sem("combT_full"), sem("combT_ready")
        var_ready, rstd_ready, res_ready = sem("c_var"), sem("c_rstd_ready"), sem("res_ready")
        dve = sem("c_dve")
        A_USES, H2_USES = DC + E * EC, (E + 1) * NT
        BIAS_AT = 3

        def h2_use(e):
            return NT * (BIAS_AT if e is None else e + (e >= BIAS_AT))

        PRODUCTS = ((0, 0), (0, 1), (1, 0))
        block = ctx.enter_context(nc.Block())

        @block.sync
        def _(sp):
            with sp.Fori(0, B) as b, sp.Fori(0, STEPS // B) as r:
                g = b * (STEPS // B) + r
                wait_apart(sp, ao_ready, 1 + g * 2, passed_sp)
                heads = scratch["av"].rearrange("(b h) q w s -> b q h w s", b=B)[bass.ds(b, 1), bass.ds(r, 1)]\
                    .rearrange("b q h w s -> (b q h) w s")
                sp.dma_start(num[:, :], heads[:, 0:KPH, :]).then_inc(ao_ld, 16)
                sp.dma_start(den[:, :], heads[:, KPH:VW, :].broadcast_to([H, KPH, ST])).then_inc(ao_ld, 16)
                wait_apart(sp, var_ready, 1 + g, passed_sp)
                sp.dma_start(x3[:, :, :], scratch["x3"][bass.ds(g, 1)].rearrange("g p n d -> p (g n) d")).then_inc(x3_ld, 16)
                wait_apart(sp, x3_ld, g * 16 + 16, passed_sp)

        @block.gpsimd
        def _(pool):
            from_one(pool, res_free)
            pool.dma_start(ob[:, :], a["L0_ffn_o_b"].rearrange("(c p) -> p c", p=P),
                           allow_slow_non_contiguous=True).then_inc(c_small, 16)
            pool.dma_start(b1[:, :, :], a["L0_ffn_b1"].rearrange("e (j p) -> p e j", p=P),
                           allow_slow_non_contiguous=True).then_inc(c_small, 16)
            for t in range(NT):
                pool.dma_start(rb[:, t, :], a["L0_ffn_router_b"].rearrange("(o n) -> o n", o=1).broadcast_to([P, E])).then_inc(c_small, 16)
            identity_matrix(pool, ident[:, :], c_made)
            pool.iota(iota_i[:, :], pattern=[[1, E]], base=0, channel_multiplier=0).then_inc(c_made, 1)
            pool.memset(minus_half[:, :], -0.5).then_inc(c_made, 1)
            pool.wait_ge(c_made, 4)
            outs = out.rearrange("b (n p) d -> p (b n) d", p=P)
            with pool.Fori(0, STEPS) as g:
                pool.wait_ge(var_ready, 1 + g + 1)
                pool.tensor_tensor(rstd[:, :], var_eps[:, :], minus_half[:, :], ALU.pow).then_inc(rstd_ready, 1)
                pool.wait_ge(res_ready, g * NT + NT)
                pool.dma_start(outs[:, bass.ds(g * NT, NT), :], res[:, :, :]).then_inc(out_stored, 16)
                pool.wait_ge(out_stored, g * 16 + 16)
                pool.sem_inc(res_free, 1)
            pool.wait_ge(out_stored, 16 * STEPS)

        @block.vector
        def _(v):
            from_one(v, ao_ready, h2_taken, var_ready, h1_split)

            own = Steps(dve, 79)
            PIECES = 2

            def step(g, instruction):
                own.mark(instruction)
                v.wait_ge(dve, own.value(g))

            def by_expert(column):
                return column.rearrange("p (t o) -> p t o", o=1).broadcast_to([P, NT, E])

            def attention_out(g, base, piece):
                v.wait_ge(ao_ld, g * 32 + 32)
                cols = slice(piece * ST // PIECES, (piece + 1) * ST // PIECES)
                step(base, v.reciprocal(den[:, cols], den[:, cols]))
                v.tensor_tensor(aoT[:, cols], num[:, cols], den[:, cols], ALU.mult).then_inc(ao_ready, 1)

            def split(base, high, low, src, done):
                step(base, v.tensor_copy(high, src))
                v.tensor_tensor(low, src, high, ALU.subtract).then_inc(done, 1)

            def split_mla(g, base):
                for c in range(DC):
                    v.wait_ge(acc_taken, g * A_USES + c + 1)
                    split(base, mla_parts[:, 0, c, :], mla_parts[:, 1, c, :], mlaT[:, c, :], mla_split)

            def split_hidden(g, e, j):
                v.wait_ge(acc_taken, g * A_USES + DC + e * EC + j + 1)
                split(g, h1[:, e % 2, 0, j, :], h1[:, e % 2, 1, j, :], gelu[:, j % 2, :], h1_split)

            def route(g, base):
                v.wait_ge(logits_full, g + 1)
                step(base, v.tensor_tensor(logits[:, :, :], R[:, 0:NT * E].rearrange("p (t e) -> p t e", t=NT), rb[:, :, :], ALU.add))
                step(base, v.tensor_reduce(small[:, :], logits[:, :, :], axis=AX.X, op=ALU.max))
                v.tensor_tensor(logits[:, :, :], logits[:, :, :], by_expert(small[:, :]), ALU.subtract).then_inc(logits_ready, 1)
                v.wait_ge(exp_ready, g + 1)
                step(base, v.tensor_reduce(small[:, :], probs[:, :, :], axis=AX.X, op=ALU.add))
                step(base, v.reciprocal(small[:, :], small[:, :]))
                own.mark(v.tensor_tensor(probs[:, :, :], probs[:, :, :], by_expert(small[:, :]), ALU.mult))
                wait_apart(v, dve, own.value(base), passed_v)
                for t in range(NT):
                    own.mark(v.max(best[:, t, :], probs[:, t, :]))
                wait_apart(v, dve, own.value(base), passed_v)
                for t in range(NT):
                    own.mark(v.max_index(best_at[:, t, :], best[:, t, :], probs[:, t, :]))
                step(base, v.tensor_tensor(weight_sum[:, :], best[:, :, 0], best[:, :, 1], ALU.add))
                step(base, v.tensor_scalar(weight_sum[:, :], weight_sum[:, :], 1e-8, None, ALU.add))
                own.mark(v.tensor_copy(at_f[:, :, :], best_at[:, :, 0:2]))
                step(base, v.reciprocal(weight_sum[:, :], weight_sum[:, :]))
                for k in range(2):
                    own.mark(v.tensor_tensor(weight[:, :, k], best[:, :, k], weight_sum[:, :], ALU.mult))
                v.wait_ge(dve, own.value(base))
                for t in range(NT):
                    for k in range(2):
                        own.mark(v.tensor_scalar(chosen[:, k, t, :], iota[:, :], at_f[:, t, k:k + 1], weight[:, t, k:k + 1],
                                                 ALU.is_equal, ALU.mult))
                v.wait_ge(dve, own.value(base))

            def combine(g, e):
                for t in range(NT):
                    use = h2_use(e) + t
                    v.wait_ge(h2_taken, 1 + g * H2_USES + max(use + 1 - NT, 0))
                    v.wait_ge(h2_full, g * H2_USES + use + 1)
                    if e is None:
                        i = v.tensor_tensor(moe[:, t, :], H2[t][:, 0:D], moe[:, t, :], ALU.add)
                    elif e == 0:
                        i = v.tensor_scalar(moe[:, t, :], H2[t][:, 0:D], comb[:, t, 0:1], None, ALU.mult)
                    else:
                        i = v.scalar_tensor_tensor(moe[:, t, :], H2[t][:, 0:D], comb[:, t, e:e + 1], moe[:, t, :],
                                                   ALU.mult, ALU.add)
                    i.then_inc(h2_taken, 1)

            def weights(g):
                v.wait_ge(h2_taken, 1 + g * H2_USES)
                v.tensor_tensor(comb[:, :, :], chosen[:, 0, :, :], chosen[:, 1, :, :], ALU.add).then_inc(comb_ready, 1)

            def layer_norm(g, base, quarter):
                if quarter == 0:
                    v.wait_ge(x3_ld, g * 16 + 16)
                    v.wait_ge(res_free, 1 + g)
                    for t in range(NT):
                        own.mark(v.scalar_tensor_tensor(res[:, t, :], moe[:, t, :], 0.3, x3[:, t, :], ALU.mult, ALU.add))
                    v.wait_ge(dve, own.value(base))
                elif quarter == 1:
                    for t in range(NT):
                        own.mark(v.tensor_tensor(res[:, t, :], res[:, t, :], x3[:, t, :], ALU.add))
                    v.wait_ge(dve, own.value(base))
                elif quarter == 2:
                    for t in range(NT):
                        own.mark(v.bn_stats(stats[:, t, :], res[:, t, :]))
                    wait_apart(v, dve, own.value(base), passed_v)
                    for t in range(NT):
                        own.mark(v.bn_aggr(meanvar[:, t, :], stats[:, t, :]))
                    v.wait_ge(dve, own.value(base))
                    v.tensor_scalar(var_eps[:, :], meanvar[:, :, 1], EPS_LN, None, ALU.add).then_inc(var_ready, 1)
                else:
                    v.wait_ge(rstd_ready, g + 1)
                    for t in range(NT):
                        v.tensor_scalar(res[:, t, :], res[:, t, :], meanvar[:, t, 0:1], rstd[:, t:t + 1],
                                        ALU.subtract, ALU.mult).then_inc(res_ready, 1)
                    v.wait_ge(res_ready, g * NT + NT)

            def body(g, first, last):
                own.n = before
                for e in range(E):
                    if e >= 2:
                        combine(g, e - 2)
                    if e == BIAS_AT:
                        v.wait_ge(combT_full, g + 1)
                        v.tensor_copy(combT[:, :], CT[0:E, :]).then_inc(combT_ready, 1)
                    for j in range(EC):
                        split_hidden(g, e, j)
                    if e < 4 and not first:
                        layer_norm(g - 1, g, e)
                    if e == BIAS_AT + 1:
                        combine(g, None)
                    if e - 4 in range(PIECES) and not last:
                        attention_out(g + 1, g, e - 4)
                combine(g, E - 2)
                if not last:
                    split_mla(g + 1, g)
                    route(g + 1, g)
                combine(g, E - 1)
                if not last:
                    weights(g + 1)
                if first:
                    v.sem_inc(dve, before + own.per - own.n)
                else:
                    assert last or own.n == before + own.per, own.n - before

            for piece in range(PIECES):
                attention_out(0, 0, piece)
            v.wait_ge(c_small, 16 * (2 + NT))
            v.wait_ge(c_made, 4)
            v.tensor_copy(iota[:, :], iota_i[:, :]).then_inc(c_made, 1)
            v.wait_ge(c_made, 5)
            split_mla(0, 0)
            route(0, 0)
            weights(0)
            before = own.n
            body(0, True, False)
            with v.Fori(1, STEPS - 1) as g:
                body(g, False, False)
            body(STEPS - 1, False, True)
            v.wait_ge(h2_taken, 1 + STEPS * H2_USES)
            for quarter in range(4):
                layer_norm(STEPS - 1, STEPS - 1, quarter)

        @block.scalar
        def _(s):
            s.dma_start(ow[:, :], a["L0_ffn_o_w"][0:LAT, :]).then_inc(c_ld, 16)
            s.dma_start(rw[:, :, :], a["L0_ffn_router_w"].rearrange("(c p) e -> p c e", p=P)).then_inc(c_ld, 16)
            s.dma_start(b2[:, :], a["L0_ffn_b2"]).then_inc(c_ld, 16)
            s.wait_ge(c_small, 16 * (2 + NT))

            def project_out(g):
                for c in range(DC):
                    s.wait_ge(acc_full, g * A_USES + c + 1)
                    s.activation(mlaT[:, c, :], A[c][:, :], ACT.Identity, bias=ob[:, c:c + 1]).then_inc(acc_taken, 1)
                s.wait_ge(logits_ready, g + 1)
                s.activation(probs[:, :, :], logits[:, :, :], ACT.Exp).then_inc(exp_ready, 1)

            def hidden(g, e):
                for j in range(EC):
                    s.wait_ge(acc_full, g * A_USES + DC + e * EC + j + 1)
                    chunk = e * EC + j
                    s.wait_ge(h1_split, 1 + g * E * EC + max(chunk - 1, 0))
                    s.activation(gelu[:, j % 2, :], A[j % 2][:, :], ACT.Gelu, bias=b1[:, e, j:j + 1]).then_inc(acc_taken, 1)

            def body(g, last):
                for e in range(E):
                    hidden(g, e)
                if not last:
                    project_out(g + 1)

            project_out(0)
            with s.Fori(0, STEPS - 1) as g:
                body(g, False)
            body(STEPS - 1, True)

        @block.tensor
        def _(pe):
            pe.wait_ge(c_ld, 16 * 3)
            pe.wait_ge(c_made, 4)

            def free_acc(g, use):
                n = g * A_USES + use - 1
                if not isinstance(g, int) or n > 0:
                    pe.wait_ge(acc_taken, n)

            def front(g):
                pe.wait_ge(ao_ready, 1 + g * 2 + 2)
                for c in range(DC):
                    free_acc(g, c)
                    pe.matmul(A[c][:, :], ow[:, c * P:(c + 1) * P], aoT[:, :], start=True, stop=True).then_inc(acc_full, 1)
                pe.wait_ge(acc_taken, g * A_USES + DC)
                if not isinstance(g, int):
                    pe.wait_ge(logits_ready, g)
                for t in range(NT):
                    for c in range(DC):
                        last = pe.matmul(R[:, t * E:(t + 1) * E], mlaT[:, c, t * P:(t + 1) * P], rw[:, c, :],
                                         start=(c == 0), stop=(c == DC - 1))
                last.then_inc(logits_full, 1)

            def hidden(g, e):
                if e == 0:
                    pe.wait_ge(mla_split, (g + 1) * DC)
                for j in range(EC):
                    free_acc(g, DC + e * EC + j)
                    for c in range(DC):
                        for i, (w, m) in enumerate(PRODUCTS):
                            last = pe.matmul(A[j % 2][:, :], w1[:, e, c, w, j * P:(j + 1) * P], mla_parts[:, m, c, :],
                                             start=(c == 0 and i == 0), stop=(c == DC - 1 and i == len(PRODUCTS) - 1))
                    last.then_inc(acc_full, 1)

            def free_h2(g, use):
                n = g * H2_USES + use - NT + 1
                if not isinstance(g, int):
                    pe.wait_ge(h2_taken, 1 + g * H2_USES + max(use - NT + 1, 0))
                elif n > 0:
                    pe.wait_ge(h2_taken, 1 + n)

            def turn_weights(g):
                pe.wait_ge(comb_ready, g + 1)
                for t in range(NT):
                    last = pe.transpose(CT[0:E, t * P:(t + 1) * P], comb[:, t, :], ident[:, :])
                last.then_inc(combT_full, 1)

            def second_biases(g):
                pe.wait_ge(combT_ready, g + 1)
                for t in range(NT):
                    free_h2(g, h2_use(None) + t)
                    pe.matmul(H2[t][:, 0:D], combT[:, t * P:(t + 1) * P], b2[:, :], start=True, stop=True).then_inc(h2_full, 1)

            def expert_out(g, e):
                pe.wait_ge(h1_split, 1 + g * E * EC + (e + 1) * EC)
                for t in range(NT):
                    free_h2(g, h2_use(e) + t)
                    for j in range(EC):
                        for i, (h, w) in enumerate(PRODUCTS):
                            last = pe.matmul(H2[t][:, 0:D], h1[:, e % 2, h, j, t * P:(t + 1) * P],
                                             w2[:, e, j // 2, w, (j % 2) * D:(j % 2 + 1) * D],
                                             start=(j == 0 and i == 0), stop=(j == EC - 1 and i == len(PRODUCTS) - 1))
                    last.then_inc(h2_full, 1)

            def body(g, last):
                hidden(g, 0)
                hidden(g, 1)
                for e in range(2, E):
                    expert_out(g, e - 2)
                    hidden(g, e)
                    if e == BIAS_AT - 1:
                        turn_weights(g)
                    if e == BIAS_AT + 1:
                        second_biases(g)
                expert_out(g, E - 2)
                if not last:
                    front(g + 1)
                expert_out(g, E - 1)

            front(0)
            with pe.Fori(0, STEPS - 1) as g:
                body(g, False)
            body(STEPS - 1, True)


def post_ln_block(nc, a, out):
    def dram(name, shape, dt=F32):
        return nc.dram_tensor(name, shape, dt).ap()

    scratch = {
        "x3": dram("x3_scratch", [STEPS, P, NT, D]),
        "v": dram("v_scratch", [P, TC, HEADS * VW]),
        "qk": dram("qk_scratch", [2, PARTS, B, LAT, T], BF16),
        "av": dram("av_scratch", [HEADS, SB, VW, 512]),
    }
    linear_attention_stage(nc, a, scratch)
    with (
        nc.sbuf_tensor("w1", [P, E, DC, 2, EF], F32R) as w1,
        nc.sbuf_tensor("w2", [P, E, 2, 2, EF], F32R) as w2,
    ):
        softmax_attention_stage(nc, a, scratch, w1, w2)
        experts_stage(nc, a, scratch, w1, w2, out)


_IN = ["L0_attn_" + n for n in ("x", "ln1_g", "ln1_b", "Wq", "Wk", "Wv", "Wo", "ln2_g", "ln2_b", "Wf1", "Wf2")] + \
      ["L0_ffn_" + n for n in ("q_w", "q_b", "k_w", "k_b", "v_w", "v_b", "o_w", "o_b", "router_w", "router_b",
                               "w1", "b1", "w2", "b2")]


def kernel(**inputs):
    import numpy as np
    import concourse.bacc as bacc
    from concourse.bass_utils import run_bass_kernel_spmd

    nc = bacc.Bacc("TRN2", target_bir_lowering=False, num_devices=1)
    arrays, aps = {}, {}
    for name in _IN:
        arrays[f"in_{name}"] = np.ascontiguousarray(inputs[name])
        aps[name] = nc.dram_tensor(f"in_{name}", arrays[f"in_{name}"].shape, F32, kind="ExternalInput").ap()
    out = nc.dram_tensor("out", [B, T, D], F32, kind="ExternalOutput").ap()
    post_ln_block(nc, aps, out)
    r = run_bass_kernel_spmd(nc, [arrays], core_ids=[0])
    return r.results[0]["out"]
```
